# Optimizing a Trainium2 kernel written in Bass

```python
import numpy as np
import jax
import jax.numpy as jnp

def _softmax(x, axis=-1):
    return jax.nn.softmax(x, axis=axis)

def _gelu(x):
    return jax.nn.gelu(x, approximate=True)

def _silu(x):
    return jax.nn.silu(x)

def _sigmoid(x):
    return jax.nn.sigmoid(x)

def _layernorm(x, axis=-1, eps=1e-05):
    m = jnp.mean(x, axis=axis, keepdims=True)
    v = jnp.var(x, axis=axis, keepdims=True)
    return (x - m) / jnp.sqrt(v + eps)

def _scatter_add(tgt, idx, src, axis=0):
    return tgt.at[idx].add(src)

def _segment_sum(src, seg, n):
    return jax.ops.segment_sum(src, seg, n)
kernel_name = 'mk_xattn_ffn_d2_seqx_r8_51dac0'

def setup_inputs(seed: int=0):
    np.random.seed(seed)
    _w = jnp.asarray

    def _rec_inputs():
        import jax
        import jax.numpy as jnp
        _rk = jax.random.key(seed)
        x = 7.22e-05 + 1 * jax.random.normal(jax.random.fold_in(_rk, 1), (128, 64, 128), jnp.float32)
        _lenS = 64 - jax.random.randint(jax.random.fold_in(_rk, 7), (128,), 0, max(1, 64 // 4) + 1, jnp.int32)
        _lenS2 = 64 - jax.random.randint(jax.random.fold_in(_rk, 8), (128,), 0, max(1, 64 // 4) + 1, jnp.int32)
        _ctx_1024P = jax.random.normal(jax.random.fold_in(_rk, 11), (128, 16, 128), jnp.float32)
        _ctx_1024c = jax.random.dirichlet(jax.random.fold_in(_rk, 511), 0.3 * jnp.ones((16,), jnp.float32), (128, 64))
        _ctx_1024t = jnp.einsum('bsk,bkd->bsd', _ctx_1024c, _ctx_1024P)
        _ctx_1024t = _ctx_1024t * jax.lax.rsqrt(jnp.mean(jnp.square(_ctx_1024t)) + 1e-12) * 0.953939
        ctx_1024 = 4.13588e-05 + 0.999923 * (_ctx_1024t + 0.3 * jax.random.normal(jax.random.fold_in(_rk, 611), (128, 64, 128), jnp.float32))
        return (x, ctx_1024)
    x, ctx_1024 = _rec_inputs()

    def _L0_xattn_setup():
        import jax, jax.numpy as jnp
        import numpy as np
        D_MODEL = 128
        N_HEADS = 16
        HEAD_DIM = D_MODEL // N_HEADS
        EPS = 1e-05

        def layer_norm(x, g, b):
            mu = jnp.mean(x, axis=-1, keepdims=True)
            var = jnp.mean(jnp.square(x - mu), axis=-1, keepdims=True)
            return (x - mu) * jax.lax.rsqrt(var + EPS) * g + b
        key = jax.random.key(seed)
        ks = jax.random.split(key, 16)
        B, S, D = (4, 256, D_MODEL)
        s = 1.0 / np.sqrt(D)
        inp = {'query': jax.random.normal(ks[0], (B, S, D), jnp.float32), 'key': jax.random.normal(ks[1], (B, S, D), jnp.float32), 'value': jax.random.normal(ks[2], (B, S, D), jnp.float32), 'Wq': jax.random.normal(ks[3], (D, D), jnp.float32) * s, 'bq': jnp.zeros((D,), jnp.float32), 'Wk': jax.random.normal(ks[4], (D, D), jnp.float32) * s, 'bk': jnp.zeros((D,), jnp.float32), 'Wv': jax.random.normal(ks[5], (D, D), jnp.float32) * s, 'bv': jnp.zeros((D,), jnp.float32), 'Wo': jax.random.normal(ks[6], (D, D), jnp.float32) * s, 'bo': jnp.zeros((D,), jnp.float32), 'Wg': jax.random.normal(ks[7], (D, 1), jnp.float32) * s, 'ln_q_g': jnp.ones((D,), jnp.float32), 'ln_q_b': jnp.zeros((D,), jnp.float32), 'ln_kv_g': jnp.ones((D,), jnp.float32), 'ln_kv_b': jnp.zeros((D,), jnp.float32), 'ln_o_g': jnp.ones((D,), jnp.float32), 'ln_o_b': jnp.zeros((D,), jnp.float32)}
        return inp
    _L0_xattn_all = _L0_xattn_setup()
    _L0_xattn_in = {k: v for k, v in _L0_xattn_all.items() if k in ('Wq', 'bq', 'Wk', 'bk', 'Wv', 'bv', 'Wo', 'bo', 'Wg', 'ln_q_g', 'ln_q_b', 'ln_kv_g', 'ln_kv_b', 'ln_o_g', 'ln_o_b')}
    del _L0_xattn_all

    def _L0_ffn_setup():
        import jax, jax.numpy as jnp
        import numpy as np
        D_IN, D_HID = (128, 512)

        def _ternary(key, shape):
            return jax.random.randint(key, shape, -1, 2).astype(jnp.float32)

        def _tlin(x, w, s):
            return jnp.einsum('bsi,oi->bso', x, w) * s
        key = jax.random.key(seed)
        ks = jax.random.split(key, 12)
        inv = lambda fan: 1.0 / np.sqrt(fan).astype(np.float32)
        return {'x': jax.random.normal(ks[0], (4, 256, D_IN), dtype=jnp.float32), 'w1_w': _ternary(ks[1], (D_HID, D_IN)), 'w1_s': jax.random.uniform(ks[2], (D_HID,), dtype=jnp.float32) * inv(D_IN), 'w2_w': _ternary(ks[3], (D_HID, D_IN)), 'w2_s': jax.random.uniform(ks[4], (D_HID,), dtype=jnp.float32) * inv(D_IN), 'h1_w': _ternary(ks[5], (D_HID, D_HID)), 'h1_s': jax.random.uniform(ks[6], (D_HID,), dtype=jnp.float32) * inv(D_HID), 'h2_w': _ternary(ks[7], (D_HID, D_HID)), 'h2_s': jax.random.uniform(ks[8], (D_HID,), dtype=jnp.float32) * inv(D_HID), 'w3_w': _ternary(ks[9], (D_IN, D_HID)), 'w3_s': jax.random.uniform(ks[10], (D_IN,), dtype=jnp.float32) * inv(D_HID)}
    _L0_ffn_all = _L0_ffn_setup()
    _L0_ffn_in = {k: v for k, v in _L0_ffn_all.items() if k in ('w1_w', 'w1_s', 'w2_w', 'w2_s', 'h1_w', 'h1_s', 'h2_w', 'h2_s', 'w3_w', 'w3_s')}
    del _L0_ffn_all

    def _L1_xattn_setup():
        import jax, jax.numpy as jnp
        import numpy as np
        D_MODEL = 128
        N_HEAD = 16

        def _split_heads(x):
            B, S, D = x.shape
            return x.reshape(B, S, N_HEAD, D // N_HEAD).transpose(0, 2, 1, 3)
        key = jax.random.key(seed)
        ks = jax.random.split(key, 11)
        B, S, D = (2, 256, D_MODEL)
        s = 1.0 / np.sqrt(D)
        inp = {'q': jax.random.normal(ks[0], (B, S, D), jnp.float32), 'k': jax.random.normal(ks[1], (B, S, D), jnp.float32), 'v': jax.random.normal(ks[2], (B, S, D), jnp.float32), 'w_q': jax.random.normal(ks[3], (D, D), jnp.float32) * s, 'b_q': jnp.zeros((D,), jnp.float32), 'w_k': jax.random.normal(ks[4], (D, D), jnp.float32) * s, 'b_k': jnp.zeros((D,), jnp.float32), 'w_v': jax.random.normal(ks[5], (D, D), jnp.float32) * s, 'b_v': jnp.zeros((D,), jnp.float32), 'w_o': jax.random.normal(ks[6], (D, D), jnp.float32) * s, 'b_o': jnp.zeros((D,), jnp.float32)}
        return inp
    _L1_xattn_all = _L1_xattn_setup()
    _L1_xattn_in = {k: v for k, v in _L1_xattn_all.items() if k in ('w_q', 'b_q', 'w_k', 'b_k', 'w_v', 'b_v', 'w_o', 'b_o')}
    del _L1_xattn_all

    def _L1_ffn_setup():
        import jax, jax.numpy as jnp
        import numpy as np
        HIDDEN = 128
        INTER = 512
        key = jax.random.key(seed)
        k1, k2, k3, k4, k5 = jax.random.split(key, 5)
        hidden_states = jax.random.normal(k1, (4, 256, HIDDEN), dtype=jnp.float32)
        W1 = jax.random.normal(k2, (HIDDEN, INTER), dtype=jnp.float32) * (1.0 / np.sqrt(HIDDEN))
        b1 = jax.random.normal(k3, (INTER,), dtype=jnp.float32) * 0.02
        W2 = jax.random.normal(k4, (INTER, HIDDEN), dtype=jnp.float32) * (1.0 / np.sqrt(INTER))
        b2 = jax.random.normal(k5, (HIDDEN,), dtype=jnp.float32) * 0.02
        return {'hidden_states': hidden_states, 'W1': W1, 'b1': b1, 'W2': W2, 'b2': b2}
    _L1_ffn_all = _L1_ffn_setup()
    _L1_ffn_in = {k: v for k, v in _L1_ffn_all.items() if k in ('W1', 'b1', 'W2', 'b2')}
    del _L1_ffn_all
    return {'x': x, 'ctx_1024': ctx_1024, 'L0_xattn_Wq': _L0_xattn_in['Wq'], 'L0_xattn_bq': _L0_xattn_in['bq'], 'L0_xattn_Wk': _L0_xattn_in['Wk'], 'L0_xattn_bk': _L0_xattn_in['bk'], 'L0_xattn_Wv': _L0_xattn_in['Wv'], 'L0_xattn_bv': _L0_xattn_in['bv'], 'L0_xattn_Wo': _L0_xattn_in['Wo'], 'L0_xattn_bo': _L0_xattn_in['bo'], 'L0_xattn_Wg': _L0_xattn_in['Wg'], 'L0_xattn_ln_q_g': _L0_xattn_in['ln_q_g'], 'L0_xattn_ln_q_b': _L0_xattn_in['ln_q_b'], 'L0_xattn_ln_kv_g': _L0_xattn_in['ln_kv_g'], 'L0_xattn_ln_kv_b': _L0_xattn_in['ln_kv_b'], 'L0_xattn_ln_o_g': _L0_xattn_in['ln_o_g'], 'L0_xattn_ln_o_b': _L0_xattn_in['ln_o_b'], 'L0_ffn_w1_w': _L0_ffn_in['w1_w'], 'L0_ffn_w1_s': _L0_ffn_in['w1_s'], 'L0_ffn_w2_w': _L0_ffn_in['w2_w'], 'L0_ffn_w2_s': _L0_ffn_in['w2_s'], 'L0_ffn_h1_w': _L0_ffn_in['h1_w'], 'L0_ffn_h1_s': _L0_ffn_in['h1_s'], 'L0_ffn_h2_w': _L0_ffn_in['h2_w'], 'L0_ffn_h2_s': _L0_ffn_in['h2_s'], 'L0_ffn_w3_w': _L0_ffn_in['w3_w'], 'L0_ffn_w3_s': _L0_ffn_in['w3_s'], 'L1_xattn_w_q': _L1_xattn_in['w_q'], 'L1_xattn_b_q': _L1_xattn_in['b_q'], 'L1_xattn_w_k': _L1_xattn_in['w_k'], 'L1_xattn_b_k': _L1_xattn_in['b_k'], 'L1_xattn_w_v': _L1_xattn_in['w_v'], 'L1_xattn_b_v': _L1_xattn_in['b_v'], 'L1_xattn_w_o': _L1_xattn_in['w_o'], 'L1_xattn_b_o': _L1_xattn_in['b_o'], 'L1_ffn_W1': _L1_ffn_in['W1'], 'L1_ffn_b1': _L1_ffn_in['b1'], 'L1_ffn_W2': _L1_ffn_in['W2'], 'L1_ffn_b2': _L1_ffn_in['b2']}

def reference(x, ctx_1024, L0_xattn_Wq, L0_xattn_bq, L0_xattn_Wk, L0_xattn_bk, L0_xattn_Wv, L0_xattn_bv, L0_xattn_Wo, L0_xattn_bo, L0_xattn_Wg, L0_xattn_ln_q_g, L0_xattn_ln_q_b, L0_xattn_ln_kv_g, L0_xattn_ln_kv_b, L0_xattn_ln_o_g, L0_xattn_ln_o_b, L0_ffn_w1_w, L0_ffn_w1_s, L0_ffn_w2_w, L0_ffn_w2_s, L0_ffn_h1_w, L0_ffn_h1_s, L0_ffn_h2_w, L0_ffn_h2_s, L0_ffn_w3_w, L0_ffn_w3_s, L1_xattn_w_q, L1_xattn_b_q, L1_xattn_w_k, L1_xattn_b_k, L1_xattn_w_v, L1_xattn_b_v, L1_xattn_w_o, L1_xattn_b_o, L1_ffn_W1, L1_ffn_b1, L1_ffn_W2, L1_ffn_b2):
    import jax
    import jax.numpy as jnp

    def _L0_xattn_ref(query, key, value, Wq, bq, Wk, bk, Wv, bv, Wo, bo, Wg, ln_q_g, ln_q_b, ln_kv_g, ln_kv_b, ln_o_g, ln_o_b):
        import jax, jax.numpy as jnp
        import numpy as np
        D_MODEL = 128
        N_HEADS = 16
        HEAD_DIM = D_MODEL // N_HEADS
        EPS = 1e-05

        def layer_norm(x, g, b):
            mu = jnp.mean(x, axis=-1, keepdims=True)
            var = jnp.mean(jnp.square(x - mu), axis=-1, keepdims=True)
            return (x - mu) * jax.lax.rsqrt(var + EPS) * g + b
        B, S, D = query.shape
        H, Hd = (N_HEADS, HEAD_DIM)
        scale = Hd ** (-0.5)
        qn = layer_norm(query, ln_q_g, ln_q_b)
        kn = layer_norm(key, ln_kv_g, ln_kv_b)
        vn = layer_norm(value, ln_kv_g, ln_kv_b)
        q = (qn @ Wq + bq).reshape(B, S, H, Hd)
        k = (kn @ Wk + bk).reshape(B, S, H, Hd)
        v = (vn @ Wv + bv).reshape(B, S, H, Hd)
        scores = jnp.einsum('bqhd,bkhd->bhqk', q, k) * scale
        attn = jax.nn.softmax(scores, axis=-1)
        out = jnp.einsum('bhqk,bkhd->bqhd', attn, v).reshape(B, S, D)
        out = out @ Wo + bo
        gate = jax.nn.sigmoid(qn @ Wg)
        out = gate * out
        out = layer_norm(out, ln_o_g, ln_o_b)
        return out

    def _L0_ffn_ref(x, w1_w, w1_s, w2_w, w2_s, h1_w, h1_s, h2_w, h2_s, w3_w, w3_s):
        import jax, jax.numpy as jnp
        import numpy as np
        D_IN, D_HID = (128, 512)

        def _ternary(key, shape):
            return jax.random.randint(key, shape, -1, 2).astype(jnp.float32)

        def _tlin(x, w, s):
            return jnp.einsum('bsi,oi->bso', x, w) * s
        h = jax.nn.silu(_tlin(x, w1_w, w1_s)) * _tlin(x, w2_w, w2_s)
        h = jax.nn.gelu(_tlin(h, h1_w, h1_s), approximate=False)
        h = jax.nn.gelu(_tlin(h, h2_w, h2_s), approximate=False)
        return _tlin(h, w3_w, w3_s)

    def _L1_xattn_ref(q, k, v, w_q, b_q, w_k, b_k, w_v, b_v, w_o, b_o):
        import jax, jax.numpy as jnp
        import numpy as np
        D_MODEL = 128
        N_HEAD = 16

        def _split_heads(x):
            B, S, D = x.shape
            return x.reshape(B, S, N_HEAD, D // N_HEAD).transpose(0, 2, 1, 3)
        qh = _split_heads(q @ w_q.T + b_q)
        kh = _split_heads(k @ w_k.T + b_k)
        vh = _split_heads(v @ w_v.T + b_v)
        d_k = qh.shape[-1]
        scores = jnp.einsum('bhqd,bhkd->bhqk', qh, kh) / jnp.sqrt(jnp.float32(d_k))
        attn = jax.nn.softmax(scores, axis=-1)
        out = jnp.einsum('bhqk,bhkd->bhqd', attn, vh)
        B, H, S, d = out.shape
        out = out.transpose(0, 2, 1, 3).reshape(B, S, H * d)
        return out @ w_o.T + b_o

    def _L1_ffn_ref(hidden_states, W1, b1, W2, b2):
        import jax, jax.numpy as jnp
        import numpy as np
        HIDDEN = 128
        INTER = 512
        h = jax.nn.relu(jnp.einsum('bsh,hi->bsi', hidden_states, W1) + b1)
        return jnp.einsum('bsi,ih->bsh', h, W2) + b2
    x = x + _L0_xattn_ref(_layernorm(x, axis=-1), ctx_1024, ctx_1024, L0_xattn_Wq, L0_xattn_bq, L0_xattn_Wk, L0_xattn_bk, L0_xattn_Wv, L0_xattn_bv, L0_xattn_Wo, L0_xattn_bo, L0_xattn_Wg, L0_xattn_ln_q_g, L0_xattn_ln_q_b, L0_xattn_ln_kv_g, L0_xattn_ln_kv_b, L0_xattn_ln_o_g, L0_xattn_ln_o_b)
    x = x + _L0_ffn_ref(_layernorm(x, axis=-1), L0_ffn_w1_w, L0_ffn_w1_s, L0_ffn_w2_w, L0_ffn_w2_s, L0_ffn_h1_w, L0_ffn_h1_s, L0_ffn_h2_w, L0_ffn_h2_s, L0_ffn_w3_w, L0_ffn_w3_s)
    x = x + _L1_xattn_ref(_layernorm(x, axis=-1), ctx_1024, ctx_1024, L1_xattn_w_q, L1_xattn_b_q, L1_xattn_w_k, L1_xattn_b_k, L1_xattn_w_v, L1_xattn_b_v, L1_xattn_w_o, L1_xattn_b_o)
    x = x + _L1_ffn_ref(_layernorm(x, axis=-1), L1_ffn_W1, L1_ffn_b1, L1_ffn_W2, L1_ffn_b2)
    return x

_drawn_inputs = setup_inputs


def setup_inputs(seed=0):
    import zlib

    import numpy as np

    out = dict(_drawn_inputs(seed))
    spreads = {'L0_xattn_bq': (0.0, 0.1),
     'L0_xattn_bk': (0.0, 0.1),
     'L0_xattn_bv': (0.0, 0.1),
     'L0_xattn_bo': (0.0, 0.1),
     'L0_xattn_ln_q_g': (1.0, 0.2),
     'L0_xattn_ln_q_b': (0.0, 0.1),
     'L0_xattn_ln_kv_g': (1.0, 0.2),
     'L0_xattn_ln_kv_b': (0.0, 0.1),
     'L0_xattn_ln_o_g': (1.0, 0.2),
     'L0_xattn_ln_o_b': (0.0, 0.1),
     'L1_xattn_b_q': (0.0, 0.1),
     'L1_xattn_b_k': (0.0, 0.1),
     'L1_xattn_b_v': (0.0, 0.1),
     'L1_xattn_b_o': (0.0, 0.1)}
    factors = {}
    for name, (base, spread) in spreads.items():
        noise = np.random.default_rng([zlib.crc32(name.encode()), seed]).standard_normal(out[name].shape)
        drawn = base * np.exp(spread * noise) if base else spread * noise
        out[name] = jnp.asarray(drawn.astype(out[name].dtype))
    for name, factor in factors.items():
        out[name] = (out[name] * factor).astype(out[name].dtype)
    return out
```

```python
from contextlib import ExitStack

import concourse.bass as bass
from concourse import mybir

ALU = mybir.AluOpType
ACT = mybir.ActivationFunctionType
AX = mybir.AxisListType
F32 = mybir.dt.float32
F32R = mybir.dt.float32r

P = 128
EPS = 1e-5
HEADS = 16
HEAD_DIM = 8
SEQ = 64
PER_TILE = P // SEQ
PAIRS = HEADS // 2
UNROLL = 4


def wait(eng, sem, count):
    if isinstance(count, int) and count <= 0:
        return
    eng.wait_ge(sem, count)


def span(i, width):
    return slice(i * width, (i + 1) * width) if isinstance(i, int) else bass.ds(i * width, width)


class Steps:

    def __init__(self, total, lead, lag, unroll):
        self.total, self.first, self.last, self.unroll = total, -lead, total + lag, unroll
        self.lo = -(-lag // unroll) * unroll
        self.hi = (total - lead) // unroll * unroll

    def run(self, eng, step):
        for j in range(self.first, self.lo):
            step(j, j % self.unroll)
        with eng.Fori(self.lo, self.hi, self.unroll) as base:
            for u in range(self.unroll):
                step(base + u, u)
        for j in range(self.hi, self.last):
            step(j, j % self.unroll)

    def on(self, i):
        return not isinstance(i, int) or 0 <= i < self.total


def column(a):
    return a.rearrange("(p a) -> p a", a=1)


def row_everywhere(a):
    return a.rearrange("(a n) -> a n", a=1).to_broadcast([P, P])


def prepare(nc, t, a):
    with ExitStack() as ctx:
        def sb(name, shape, dt=F32):
            return ctx.enter_context(nc.sbuf_tensor(name, shape, dt))

        def sem(name):
            return ctx.enter_context(nc.semaphore(name))

        raw = sb("raw_ffn0", [P, 11, 4, P])
        raw_l1 = sb("raw_l1", [P, 4, P])
        raw_l0 = sb("raw_l0", [P, 4, P])
        raw_w1 = sb("raw_w1", [P, 4, P])
        raw_w2 = sb("raw_w2", [P, 4, P])
        cols = sb("cols", [P, 10])
        rows = sb("rows", [P, 3, P])
        sums = sb("sums", [P, 4])
        vb = sb("vb", [P, 2])
        vb_wide = sb("vb_wide", [P, 2, P])
        ps = ctx.enter_context(nc.psum_tensor("prep_ps", [P, 4, 512], F32))
        ps_b = ctx.enter_context(nc.psum_tensor("prep_ps_b", [P, 512], F32))
        ps_r = ctx.enter_context(nc.psum_tensor("prep_ps_r", [P, 2, 512], F32))

        ld_small, ld_l, ld_x, ld_c = sem("ld_small"), sem("ld_l"), sem("ld_x"), sem("ld_c")
        ld_raw = [sem(f"ld_raw{g}") for g in range(5)]
        ld_w = sem("ld_w")
        ident_zero, ident_ready, consts_ready = sem("ident_zero"), sem("ident_ready"), sem("consts_ready")
        turned = sem("turned")
        hi_taken, lo_taken = sem("hi_taken"), sem("lo_taken")
        l1_taken = sem("l1_taken")
        bias_ps, bias_row_ps = sem("bias_ps"), sem("bias_row_ps")
        vb_ready = sem("vb_ready")
        chain = sem("prep_chain")
        scaled = sem("prep_scaled")

        XQ = 4
        NT = t.tiles // XQ
        GROUPS = [("w1", 0), ("w2", 0)] + [("h1", c) for c in range(4)] + [("h2", c) for c in range(4)] + [("w3", 0)]

        with nc.Block() as block:
            @block.sync
            def _(sp):
                sp.dma_start(raw_l0[:, 0, :], a["L0_xattn_Wq"]).then_inc(ld_l, 16)
                sp.dma_start(raw_l0[:, 1, :], a["L0_xattn_Wk"]).then_inc(ld_l, 16)
                sp.dma_start(raw_l0[:, 2, :], a["L0_xattn_Wv"]).then_inc(ld_l, 16)
                sp.dma_start(raw_l0[:, 3, :], a["L0_xattn_Wo"]).then_inc(ld_l, 16)
                for n, k in enumerate(("w_q", "w_k", "w_v", "w_o")):
                    sp.dma_start(raw_l1[:, n, :], a[f"L1_xattn_{k}"]).then_inc(ld_l, 16)
                xv = a["x"].rearrange("(t b) s d -> (b s) t d", b=PER_TILE)
                cv = a["ctx_1024"].rearrange("(t b) s d -> (b s) t d", b=PER_TILE)
                xs = t.x[:, :].rearrange("p (t d) -> p t d", d=P)
                cs = t.ctx[:, :].rearrange("p (t d) -> p t d", d=P)
                for n in range(XQ):
                    sp.dma_start(xs[:, n * NT:(n + 1) * NT, :], xv[:, n * NT:(n + 1) * NT, :]).then_inc(ld_x, 16)
                    sp.dma_start(cs[:, n * NT:(n + 1) * NT, :], cv[:, n * NT:(n + 1) * NT, :]).then_inc(ld_c, 16)
                sp.wait_ge(ld_x, 16 * XQ)
                sp.wait_ge(ld_c, 16 * XQ)

            @block.scalar
            def _(act):
                names = ["L0_xattn_bq", "L0_xattn_bk", "L0_xattn_bv", "L0_xattn_ln_q_g", "L0_xattn_ln_q_b",
                         "L0_xattn_ln_kv_g", "L0_xattn_ln_kv_b", "L1_xattn_b_q", "L1_xattn_b_k", "L1_xattn_b_v"]
                for n, k in enumerate(names):
                    act.dma_start(cols[:, n:n + 1], column(a[k])).then_inc(ld_small, 16)
                act.dma_start(rows[:, 0, :], row_everywhere(a["L0_xattn_Wg"].rearrange("d a -> (d a)"))).then_inc(ld_small, 16)
                act.dma_start(rows[:, 1, :], row_everywhere(a["L0_xattn_ln_q_g"])).then_inc(ld_small, 16)
                act.dma_start(rows[:, 2, :], row_everywhere(a["L0_xattn_ln_q_b"])).then_inc(ld_small, 16)
                act.dma_start(t.bias_row[:, 0, :], row_everywhere(a["L0_xattn_bo"])).then_inc(ld_small, 16)
                act.dma_start(t.bias_row[:, 1, :], row_everywhere(a["L1_xattn_b_o"])).then_inc(ld_small, 16)
                act.dma_start(t.ln_o_g[:, :], row_everywhere(a["L0_xattn_ln_o_g"])).then_inc(ld_small, 16)
                act.dma_start(t.ln_o_b[:, :], row_everywhere(a["L0_xattn_ln_o_b"])).then_inc(ld_small, 16)
                for n, k in enumerate(("w1_s", "w2_s", "h1_s", "h2_s")):
                    act.dma_start(t.s[:, n, :], a[f"L0_ffn_{k}"].rearrange("(o p) -> p o", p=P),
                                  allow_slow_non_contiguous=True).then_inc(ld_small, 16)
                act.dma_start(t.s3[:, :], column(a["L0_ffn_w3_s"])).then_inc(ld_small, 16)
                act.dma_start(t.b1[:, :], a["L1_ffn_b1"].rearrange("(o p) -> p o", p=P),
                              allow_slow_non_contiguous=True).then_inc(ld_small, 16)
                act.dma_start(t.b2[:, :], column(a["L1_ffn_b2"])).then_inc(ld_small, 16)
                for g in range(11):
                    act.wait_ge(turned, g + 1)
                    act.activation(t.w_hi[:, g, :], ps[:, g % 4, :], ACT.Copy).then_inc(hi_taken, 1)
                act.wait_ge(turned, 12)
                for n in (0, 1, 3):
                    act.activation(t.wa[:, 1, n, :], ps[:, 3, n * P:(n + 1) * P], ACT.Copy)
                act.activation(t.wa[:, 1, 2, :].rearrange("p (q c d) -> p q c d", q=2, d=HEAD_DIM),
                               ps[:, 3, 2 * P:3 * P].rearrange("p (c q d) -> p q c d", q=2, d=HEAD_DIM), ACT.Copy).then_inc(l1_taken, 1)
                act.wait_ge(ld_w, 32)
                act.activation(t.f1_hi[:, 0, :], raw_w1[:, :, :], ACT.Copy)
                act.activation(t.f1_hi[:, 1, :], raw_w2[:, :, :], ACT.Copy).then_inc(hi_taken, 1)

            @block.gpsimd
            def _(pool):
                pool.dma_start(raw[:, 0, :, :], a["L0_ffn_w1_w"].rearrange("(r p) i -> p r i", p=P)).then_inc(ld_raw[0], 16)
                pool.dma_start(raw[:, 1, :, :], a["L0_ffn_w2_w"].rearrange("(r p) i -> p r i", p=P)).then_inc(ld_raw[1], 16)
                for g0, k, s in ((2, "h1_w", 2), (6, "h2_w", 3)):
                    for c in range(4):
                        pool.dma_start(raw[:, g0 + c, :, :], a[f"L0_ffn_{k}"][:, c * P:(c + 1) * P]
                                       .rearrange("(r p) i -> p r i", p=P)).then_inc(ld_raw[s], 16)
                pool.dma_start(raw[:, 10, :, :], a["L0_ffn_w3_w"].rearrange("p (c i) -> p c i", i=P)).then_inc(ld_raw[4], 16)
                pool.dma_start(raw_w1[:, :, :], a["L1_ffn_W1"].rearrange("p (o i) -> p o i", i=P)).then_inc(ld_w, 16)
                pool.dma_start(raw_w2[:, :, :], a["L1_ffn_W2"].rearrange("(c p) o -> p c o", p=P)).then_inc(ld_w, 16)
                nc.gpsimd.memset(t.ident[:, :], 0.0).then_inc(ident_zero, 1)
                nc.gpsimd.memset(t.head_mask[:, :], 1.0).then_inc(ident_zero, 1)
                nc.gpsimd.memset(t.ones_of_pair[:, :, :], 0.0).then_inc(ident_zero, 1)
                nc.gpsimd.memset(t.minus_half[:, :], -0.5)
                nc.gpsimd.memset(t.v_by_pair[:, :, :, :], 0.0)
                pool.wait_ge(ident_zero, 3)
                nc.gpsimd.affine_select(out=t.ident[:, :], in_=t.ident[:, :], compare_op=ALU.not_equal, fill=1.0,
                                        base=0, pattern=[[-1, P]], channel_multiplier=1).then_inc(ident_ready, 1)
                nc.gpsimd.affine_select(out=t.head_mask[:, :], in_=t.head_mask[:, :], compare_op=ALU.is_ge, fill=0.0,
                                        base=0, pattern=[[-HEAD_DIM, HEADS]], channel_multiplier=1).then_inc(consts_ready, 1)
                pool.wait_ge(consts_ready, 1)
                nc.gpsimd.affine_select(out=t.head_mask[:, :], in_=t.head_mask[:, :], compare_op=ALU.is_ge, fill=0.0,
                                        base=HEAD_DIM - 1, pattern=[[HEAD_DIM, HEADS]], channel_multiplier=-1).then_inc(consts_ready, 1)

            @block.tensor
            def _(pe):
                pe.wait_ge(ld_l, 128)
                pe.wait_ge(ld_small, 16 * 24)
                nc.tensor.matmul(ps_b[:, 0:1], raw_l0[:, 0, :], cols[:, 4:5], start=True, stop=True)
                nc.tensor.matmul(ps_b[:, 1:2], raw_l0[:, 1, :], cols[:, 6:7], start=True, stop=True)
                nc.tensor.matmul(ps_b[:, 2:3], raw_l0[:, 2, :], cols[:, 6:7], start=True, stop=True).then_inc(bias_ps, 1)
                pe.wait_ge(ident_ready, 1)
                for g in range(11):
                    which = g if g < 2 else 2 if g < 6 else 3 if g < 10 else 4
                    pe.wait_ge(ld_raw[which], 64 if which in (2, 3) else 16)
                    if g >= 4:
                        pe.wait_ge(hi_taken, g - 3)
                        pe.wait_ge(lo_taken, g - 3)
                    for r in range(4):
                        last = nc.tensor.transpose(ps[:, g % 4, r * P:(r + 1) * P], raw[:, g, r, :], t.ident[:, :])
                    last.then_inc(turned, 1)
                pe.wait_ge(hi_taken, 8)
                pe.wait_ge(lo_taken, 8)
                for r in range(4):
                    last = nc.tensor.transpose(ps[:, 3, r * P:(r + 1) * P], raw_l1[:, r, :], t.ident[:, :])
                last.then_inc(turned, 1)
                pe.wait_ge(vb_ready, 1)
                nc.tensor.matmul(ps_r[:, 0, 0:P], vb_wide[:, 0, :], raw_l0[:, 3, :], start=True, stop=True)
                pe.wait_ge(l1_taken, 1)
                nc.tensor.matmul(ps_r[:, 1, 0:P], vb_wide[:, 1, :], t.wa[:, 1, 3, :], start=True, stop=True).then_inc(bias_row_ps, 1)

            @block.vector
            def _(dve):
                s = float(HEAD_DIM) ** -0.5
                dve.wait_ge(ident_zero, 3)
                for parity in range(2):
                    for h2 in range(2):
                        c0 = parity * 16 + h2 * HEAD_DIM
                        nc.vector.memset(t.ones_of_pair[h2 * SEQ:(h2 + 1) * SEQ, parity, c0:c0 + HEAD_DIM], 1.0)
                dve.wait_ge(ld_l, 128)
                dve.wait_ge(ld_small, 16 * 24)
                nc.vector.tensor_scalar(t.wa[:, 0, 0, :], raw_l0[:, 0, :], cols[:, 3:4], s, ALU.mult, ALU.mult)
                nc.vector.tensor_scalar(t.wa[:, 0, 1, :], raw_l0[:, 1, :], cols[:, 5:6], None, ALU.mult)
                by_half = "p (q c d) -> p q c d", "p (c q d) -> p q c d"
                nc.vector.tensor_scalar(t.wa[:, 0, 2, :].rearrange(by_half[0], q=2, d=HEAD_DIM),
                                        raw_l0[:, 2, :].rearrange(by_half[1], q=2, d=HEAD_DIM), cols[:, 5:6], None, ALU.mult)
                nc.vector.tensor_copy(t.wa[:, 0, 3, :], raw_l0[:, 3, :])
                nc.vector.tensor_tensor(t.gate_w[:, :], rows[:, 0, :], rows[:, 1, :], ALU.mult)
                nc.vector.tensor_tensor_reduce(out=vb_wide[:, 0, :], in0=rows[:, 0, :], in1=rows[:, 2, :], scale=1.0, scalar=0.0,
                                               op0=ALU.mult, op1=ALU.add, accum_out=sums[:, 0:1]).then_inc(chain, 1)
                dve.wait_ge(chain, 1)
                nc.vector.tensor_scalar(t.gate_nb[:, :], sums[:, 0:1], -1.0, None, ALU.mult)
                dve.wait_ge(bias_ps, 1)
                nc.vector.tensor_tensor(sums[:, 1:2], ps_b[:, 0:1], cols[:, 0:1], ALU.add)
                nc.vector.tensor_tensor(t.qk_bias[:, 0, 1:2], ps_b[:, 1:2], cols[:, 1:2], ALU.add)
                nc.vector.tensor_tensor(vb[:, 0:1], ps_b[:, 2:3], cols[:, 2:3], ALU.add)
                nc.vector.tensor_copy(vb[:, 1:2], cols[:, 9:10])
                nc.vector.tensor_scalar(t.qk_bias[:, 1, 0:1], cols[:, 7:8], s, None, ALU.mult)
                nc.vector.tensor_copy(t.qk_bias[:, 1, 1:2], cols[:, 8:9]).then_inc(chain, 1)
                dve.wait_ge(chain, 2)
                nc.vector.tensor_scalar(t.qk_bias[:, 0, 0:1], sums[:, 1:2], s, None, ALU.mult)
                nc.vector.tensor_copy(vb_wide[:, :, :], vb[:, :].unsqueeze(2).to_broadcast([P, 2, P])).then_inc(vb_ready, 1)
                for g in range(11):
                    dve.wait_ge(hi_taken, g + 1)
                    nc.vector.tensor_tensor(t.w_lo[:, g, :], ps[:, g % 4, :], t.w_hi[:, g, :].bitcast(F32), ALU.subtract).then_inc(lo_taken, 1)
                dve.wait_ge(hi_taken, 12)
                nc.vector.tensor_tensor(t.f1_lo[:, 0, :], raw_w1[:, :, :].rearrange("p o i -> p (o i)"),
                                        t.f1_hi[:, 0, :].bitcast(F32), ALU.subtract)
                nc.vector.tensor_tensor(t.f1_lo[:, 1, :], raw_w2[:, :, :].rearrange("p o i -> p (o i)"),
                                        t.f1_hi[:, 1, :].bitcast(F32), ALU.subtract)
                dve.wait_ge(bias_row_ps, 1)
                nc.vector.tensor_tensor(t.bias_row[:, 0, :], t.bias_row[:, 0, :], ps_r[:, 0, 0:P], ALU.add)
                nc.vector.tensor_tensor(t.bias_row[:, 1, :], t.bias_row[:, 1, :], ps_r[:, 1, 0:P], ALU.add)
                nc.vector.tensor_scalar(t.wa[:, 1, 0, :], t.wa[:, 1, 0, :], s, None, ALU.mult)


def attention(nc, t, layer):
    gated = layer == 0
    T = t.tiles
    steps = Steps(T, lead=5, lag=5, unroll=UNROLL)
    on = steps.on
    wq, wk, wv, wo = (t.wa[:, layer, n, :] for n in range(4))

    with ExitStack() as ctx:
        def sb(name, shape, dt=F32):
            return ctx.enter_context(nc.sbuf_tensor(f"{name}{layer}", shape, dt))

        def psum(name, n=1):
            return ctx.enter_context(nc.psum_tensor(f"{name}{layer}", [P, 512 * n], F32))

        def sem(name):
            return ctx.enter_context(nc.semaphore(f"{name}{layer}"))

        stats = sb("stats", [P, UNROLL, 2, 6])
        moments = sb("moments", [P, UNROLL, 2, 2])
        spread = sb("spread", [P, UNROLL, 2])
        rstd = sb("rstd", [P, UNROLL, 2])
        normed = sb("normed", [P, UNROLL, 2, P])
        turned = sb("turned", [P, 2, 2, P])
        q_t = sb("q_t", [P, UNROLL, P])
        k_t = sb("k_t", [P, UNROLL, P])
        k_heads = sb("k_heads", [P, 2, HEADS, P])
        top = sb("top", [P, 2, HEADS])
        prob = sb("prob", [P, 2, HEADS * SEQ])
        prob_t = sb("prob_t", [P, 2, PAIRS, P])
        rden = sb("rden", [P, P])
        out_t = sb("out_t", [P, 2, P])
        if gated:
            gate_in = sb("gate_in", [P, UNROLL])
            gate_exp = sb("gate_exp", [P, UNROLL])
            gate = sb("gate", [P, UNROLL])
            gate_prod = sb("gate_prod", [P, P])
            y = sb("y", [P, 2, P])
            y_stats = sb("y_stats", [P, 6])
            y_moments = sb("y_moments", [P, UNROLL, 2])
            y_tmp = sb("y_tmp", [P, UNROLL])
            y_spread = sb("y_spread", [P, UNROLL])
            y_rstd = sb("y_rstd", [P, UNROLL])
            y_scale = sb("y_scale", [P, 1])
            y_gain = sb("y_gain", [P, P])

        ps_s = psum("ps_s", 2)
        ps_pt = psum("ps_pt", 2)
        ps_in = psum("ps_in")
        ps_qkv = psum("ps_qkv")
        ps_o = psum("ps_o")
        ps_y = psum("ps_y")

        ln_chain = sem("ln_chain")
        spread_ready = sem("spread_ready")
        rstd_ready = sem("rstd_ready")
        norm_ready = sem("norm_ready")
        ctx_ready = sem("ctx_ready")
        in_t_done = sem("in_t_done")
        in_t_taken = sem("in_t_taken")
        qkv_done = sem("qkv_done")
        k_taken = sem("k_taken")
        qkv_taken = sem("qkv_taken")
        k_heads_ready = sem("k_heads_ready")
        scores_done = sem("scores_done")
        top_ready = sem("top_ready")
        shifted = sem("shifted")
        exp_done = sem("exp_done")
        prob_t_done = sem("prob_t_done")
        prob_t_taken = sem("prob_t_taken")
        pv_done = sem("pv_done")
        rden_ready = sem("rden_ready")
        out_t_ready = sem("out_t_ready")
        y_done = sem("y_done")
        y_taken = sem("y_taken")
        biased = sem("biased")
        z_prod = sem("z_prod")
        z_ready = sem("z_ready")
        gate_exp_ready = sem("gate_exp_ready")
        y_chain = sem("y_chain")
        y_spread_ready = sem("y_spread_ready")
        y_rstd_ready = sem("y_rstd_ready")
        y2_chain = sem("y2_chain")
        x_done = sem("x_done")

        closing_row = t.ln_o_b[:, :] if gated else t.bias_row[:, 1, :]

        with nc.Block() as block:
            @block.tensor
            def _(pe):
                def step(j, u):
                    if on(j):
                        wait(pe, qkv_taken, j + 1)
                        wait(pe, k_heads_ready, j + 1)
                        wait(pe, shifted, j)
                        for half in range(2):
                            for b in range(PER_TILE):
                                last = nc.tensor.matmul(
                                    ps_s[b * SEQ:(b + 1) * SEQ, half * 512:(half + 1) * 512],
                                    q_t[:, u, b * SEQ:(b + 1) * SEQ],
                                    k_heads[:, u % 2, half * 8:(half + 1) * 8, b * SEQ:(b + 1) * SEQ],
                                    start=True, stop=True)
                        last.then_inc(scores_done, 1)
                    i, s = j + 3, (u + 3) % UNROLL
                    if on(i):
                        wait(pe, norm_ready, i + 1)
                        if not gated:
                            wait(pe, ctx_ready, i + 1)
                        wait(pe, in_t_taken, i)
                        for n in range(2):
                            last = nc.tensor.transpose(ps_in[:, n * P:(n + 1) * P], normed[:, s, n, :], t.ident[:, :])
                        last.then_inc(in_t_done, 1)
                    i, s = j - 1, (u - 1) % UNROLL
                    if on(i):
                        wait(pe, exp_done, i + 1)
                        wait(pe, prob_t_taken, i)
                        for hp in range(PAIRS):
                            last = nc.tensor.transpose(ps_pt[:, hp * P:(hp + 1) * P],
                                                       prob[:, s % 2, hp * P:(hp + 1) * P], t.ident[:, :])
                        last.then_inc(prob_t_done, 1)
                    i, s = j + 2, (u + 2) % UNROLL
                    if on(i):
                        wait(pe, in_t_taken, i + 1)
                        wait(pe, qkv_taken, i)
                        nc.tensor.matmul(ps_qkv[:, P:2 * P], wk, turned[:, s % 2, 1, :], start=True, stop=True)
                        nc.tensor.matmul(ps_qkv[:, 0:P], wq, turned[:, s % 2, 0, :], start=True, stop=True)
                        for b in range(PER_TILE):
                            for h2 in range(2):
                                last = nc.tensor.matmul(
                                    ps_qkv[h2 * SEQ:(h2 + 1) * SEQ, 2 * P + b * SEQ:2 * P + (b + 1) * SEQ],
                                    turned[:, s % 2, 1, b * SEQ:(b + 1) * SEQ],
                                    wv[:, h2 * SEQ:(h2 + 1) * SEQ], start=True, stop=True)
                        last.then_inc(qkv_done, 1)
                    i, s = j - 1, (u - 1) % UNROLL
                    if on(i):
                        wait(pe, prob_t_taken, i + 1)
                        wait(pe, out_t_ready, i)
                        for b in range(PER_TILE):
                            for parity in range(2):
                                for c in range(4):
                                    hp = 2 * c + parity
                                    nc.tensor.matmul(ps_o[32 * c:32 * c + 32, b * SEQ:(b + 1) * SEQ],
                                                     t.v_by_pair[:, s, 4 * b + c, parity * 32:parity * 32 + 32],
                                                     prob_t[:, s % 2, hp, b * SEQ:(b + 1) * SEQ],
                                                     start=(parity == 0), stop=(parity == 1))
                        for parity in range(2):
                            for c in range(4):
                                last = nc.tensor.matmul(ps_o[32 * c:32 * c + 32, P:2 * P],
                                                        t.ones_of_pair[:, parity, :],
                                                        prob_t[:, s % 2, 2 * c + parity, :],
                                                        start=(parity == 0), stop=(parity == 1))
                        last.then_inc(pv_done, 1)
                    i, s = j - 2, (u - 2) % UNROLL
                    if on(i):
                        wait(pe, out_t_ready, i + 1)
                        wait(pe, y_taken, i)
                        nc.tensor.matmul(ps_y[:, 0:P], out_t[:, s % 2, :], wo, start=True, stop=True).then_inc(y_done, 1)

                steps.run(pe, step)

            @block.scalar
            def _(act):
                def step(j, u):
                    if not gated and on(j + 4):
                        i, s = j + 4, u
                        wait(act, in_t_done, i - 3)
                        nc.scalar.activation(normed[:, s, 1, :], t.ctx[:, span(i, P)], ACT.Copy).then_inc(ctx_ready, 1)
                    i, s = j + 3, (u + 3) % UNROLL
                    if on(i):
                        wait(act, in_t_done, i + 1)
                        wait(act, qkv_done, i - 1)
                        nc.scalar.activation(turned[:, s % 2, :, :], ps_in[:, 0:2 * P].rearrange("p (n d) -> p n d", n=2),
                                             ACT.Copy).then_inc(in_t_taken, 1)
                    i, s = j - 1, (u - 1) % UNROLL
                    if on(i):
                        wait(act, prob_t_done, i + 1)
                        wait(act, pv_done, i - 1)
                        nc.scalar.activation(prob_t[:, s % 2, :, :], ps_pt[:, :].rearrange("p (n d) -> p n d", n=PAIRS),
                                             ACT.Copy).then_inc(prob_t_taken, 1)
                    i, s = j + 2, (u + 2) % UNROLL
                    if on(i):
                        wait(act, qkv_done, i + 1)
                        wait(act, k_heads_ready, i - 3)
                        nc.scalar.activation(k_t[:, s, :], ps_qkv[:, P:2 * P], ACT.Identity,
                                             bias=t.qk_bias[:, layer, 1:2]).then_inc(k_taken, 1)
                        wait(act, scores_done, i - 3)
                        nc.scalar.activation(q_t[:, s, :], ps_qkv[:, 0:P], ACT.Identity,
                                             bias=t.qk_bias[:, layer, 0:1], scale=1.0)
                        wait(act, pv_done, i - 3)
                        for h2 in range(2):
                            rows = slice(h2 * SEQ, (h2 + 1) * SEQ)
                            src = ps_qkv[rows, 2 * P:3 * P].rearrange("p (c r d) -> p c r d", r=2, d=HEAD_DIM)
                            dst = t.v_by_pair[rows, s, :, :].rearrange("p c (r q) -> p c r q", r=2)
                            last = nc.scalar.activation(dst[:, :, :, h2 * HEAD_DIM:(h2 + 1) * HEAD_DIM], src, ACT.Copy)
                        last.then_inc(qkv_taken, 1)
                    if on(j):
                        wait(act, shifted, j + 1)
                        nc.scalar.activation(prob[:, u % 2, :], prob[:, u % 2, :], ACT.Exp).then_inc(exp_done, 1)
                        if gated:
                            wait(act, z_ready, j + 1)
                            wait(act, y_spread_ready, j - 3)
                            nc.scalar.activation(gate_exp[:, u:u + 1], gate_in[:, u:u + 1], ACT.Exp, scale=-1.0,
                                                 bias=t.gate_nb[:, 0:1]).then_inc(gate_exp_ready, 1)

                steps.run(act, step)

            @block.gpsimd
            def _(pool):
                def step(j, u):
                    i, s = j + 1, (u + 1) % UNROLL
                    if on(i):
                        wait(pool, k_taken, i + 1)
                        wait(pool, scores_done, i - 1)
                        nc.gpsimd.tensor_tensor(k_heads[:, s % 2, :, :],
                                                k_t[:, s, :].unsqueeze(1).to_broadcast([P, HEADS, P]),
                                                t.head_mask[:, :].unsqueeze(2).to_broadcast([P, HEADS, P]),
                                                ALU.mult).then_inc(k_heads_ready, 1)
                    i, s = j + 5, (u + 5) % UNROLL
                    if on(i):
                        wait(pool, spread_ready, i + 1)
                        wait(pool, norm_ready, i - 3)
                        n = 2 if gated else 1
                        nc.gpsimd.tensor_tensor(rstd[:, s, 0:n], spread[:, s, 0:n], t.minus_half[:, 0:n],
                                                ALU.pow).then_inc(rstd_ready, 1)
                    i, s = j - 3, (u - 3) % UNROLL
                    if gated and on(i):
                        wait(pool, y_spread_ready, i + 1)
                        wait(pool, x_done, i - 3)
                        nc.gpsimd.tensor_tensor(y_rstd[:, s:s + 1], y_spread[:, s:s + 1], t.minus_half[:, 0:1],
                                                ALU.pow).then_inc(y_rstd_ready, 1)
                    if on(j):
                        wait(pool, norm_ready, j + 1)
                        nc.gpsimd.tensor_tensor(t.x[:, span(j, P)], t.x[:, span(j, P)], closing_row, ALU.add).then_inc(biased, 1)

                steps.run(pool, step)

            @block.vector
            def _(dve):
                def step(j, u):
                    i, s = j - 2, (u - 2) % UNROLL
                    if on(i):
                        wait(dve, pv_done, i + 1)
                        wait(dve, y_done, i - 1)
                        nc.vector.reciprocal(rden[:, :], ps_o[:, P:2 * P]).then_inc(rden_ready, 1)
                        wait(dve, rden_ready, i + 1)
                        nc.vector.tensor_tensor(out_t[:, s % 2, :], ps_o[:, 0:P], rden[:, :], ALU.mult).then_inc(out_t_ready, 1)
                    i, s = j + 5, (u + 5) % UNROLL
                    if on(i):
                        n = 2 if gated else 1
                        src = (t.x[:, span(i, P)], t.ctx[:, span(i, P)])
                        for k in range(n):
                            last = nc.vector.bn_stats(stats[:, s, k, :], src[k])
                        last.then_inc(ln_chain, 1)
                    if gated and on(j):
                        wait(dve, gate_exp_ready, j - 3)
                        nc.vector.tensor_tensor_reduce(out=gate_prod[:, :], in0=normed[:, u, 0, :], in1=t.gate_w[:, :],
                                                       scale=1.0, scalar=0.0, op0=ALU.mult, op1=ALU.add,
                                                       accum_out=gate_in[:, u:u + 1]).then_inc(z_ready, 1)
                    i, s = j + 5, (u + 5) % UNROLL
                    if on(i):
                        wait(dve, ln_chain, 2 * i + 1)
                    if on(j):
                        wait(dve, scores_done, j + 1)
                        nc.vector.tensor_reduce(out=top[:, u % 2, :], in_=ps_s[:, :].rearrange("p (h k) -> p h k", h=HEADS),
                                                op=ALU.max, axis=AX.X).then_inc(top_ready, 1)
                    if on(i):
                        for k in range(2 if gated else 1):
                            last = nc.vector.bn_aggr(moments[:, s, k, :], stats[:, s, k, :])
                        last.then_inc(ln_chain, 1)
                    if on(j):
                        wait(dve, top_ready, j + 1)
                        wait(dve, prob_t_done, j - 1)
                        nc.vector.tensor_tensor(prob[:, u % 2, :].rearrange("p (h k) -> p h k", h=HEADS),
                                                ps_s[:, :].rearrange("p (h k) -> p h k", h=HEADS),
                                                top[:, u % 2, :].unsqueeze(2).to_broadcast([P, HEADS, SEQ]),
                                                ALU.subtract).then_inc(shifted, 1)
                    if on(i):
                        wait(dve, ln_chain, 2 * i + 2)
                        wait(dve, rstd_ready, i - 3)
                        if gated:
                            nc.vector.tensor_scalar(spread[:, s, 0:1], moments[:, s, 0, 1:2], 1.0 + EPS, EPS * EPS, ALU.mult, ALU.add)
                            nc.vector.tensor_scalar(spread[:, s, 1:2], moments[:, s, 1, 1:2], EPS, None, ALU.add).then_inc(spread_ready, 1)
                        else:
                            nc.vector.tensor_scalar(spread[:, s, 0:1], moments[:, s, 0, 1:2], EPS, None, ALU.add).then_inc(spread_ready, 1)
                    i, s = j + 4, u
                    if on(i):
                        wait(dve, rstd_ready, i + 1)
                        wait(dve, in_t_done, i - 3)
                        src = (t.x[:, span(i, P)], t.ctx[:, span(i, P)])
                        for k in range(2 if gated else 1):
                            last = nc.vector.tensor_scalar(normed[:, s, k, :], src[k], moments[:, s, k, 0:1],
                                                           rstd[:, s, k:k + 1], ALU.subtract, ALU.mult)
                        last.then_inc(norm_ready, 1)
                    i, s = j - 4, u
                    if gated and on(i):
                        wait(dve, y_rstd_ready, i + 1)
                        wait(dve, biased, i + 1)
                        nc.vector.tensor_tensor(y_scale[:, 0:1], y_rstd[:, s:s + 1], gate[:, s:s + 1], ALU.mult)
                        nc.vector.scalar_tensor_tensor(out=y_gain[:, :], in0=y[:, s % 2, :], scalar=y_moments[:, s, 0:1],
                                                       in1=t.ln_o_g[:, :], op0=ALU.subtract, op1=ALU.mult).then_inc(y2_chain, 1)
                        wait(dve, y2_chain, i + 1)
                        nc.vector.scalar_tensor_tensor(out=t.x[:, span(i, P)], in0=y_gain[:, :], scalar=y_scale[:, 0:1],
                                                       in1=t.x[:, span(i, P)], op0=ALU.mult, op1=ALU.add).then_inc(x_done, 1)
                    i, s = j - 3, (u - 3) % UNROLL
                    if gated and on(i):
                        wait(dve, y_done, i + 1)
                        nc.vector.tensor_tensor(y[:, s % 2, :], ps_y[:, 0:P], t.bias_row[:, 0, :], ALU.add).then_inc(y_taken, 1)
                        wait(dve, gate_exp_ready, i + 1)
                        nc.vector.tensor_scalar(gate[:, s:s + 1], gate_exp[:, s:s + 1], 1.0, None, ALU.add).then_inc(y_chain, 1)
                        wait(dve, y_taken, i + 1)
                        nc.vector.bn_stats(y_stats[:, :], y[:, s % 2, :]).then_inc(y_chain, 1)
                        wait(dve, y_chain, 5 * i + 2)
                        nc.vector.reciprocal(gate[:, s:s + 1], gate[:, s:s + 1]).then_inc(y_chain, 1)
                        nc.vector.bn_aggr(y_moments[:, s, :], y_stats[:, :]).then_inc(y_chain, 1)
                        wait(dve, y_chain, 5 * i + 4)
                        nc.vector.tensor_scalar(y_tmp[:, s:s + 1], y_moments[:, s, 1:2], gate[:, s:s + 1], gate[:, s:s + 1],
                                                ALU.mult, ALU.mult).then_inc(y_chain, 1)
                        wait(dve, y_chain, 5 * i + 5)
                        wait(dve, y_rstd_ready, i - 3)
                        nc.vector.tensor_scalar(y_spread[:, s:s + 1], y_tmp[:, s:s + 1], EPS, None, ALU.add).then_inc(y_spread_ready, 1)
                    if not gated and on(i):
                        wait(dve, y_done, i + 1)
                        wait(dve, biased, i + 1)
                        nc.vector.tensor_tensor(t.x[:, span(i, P)], ps_y[:, 0:P], t.x[:, span(i, P)], ALU.add).then_inc(y_taken, 1)

                steps.run(dve, step)


def split_products(nc, out, w_hi, w_lo, x_hi, x_lo, first, last):
    nc.tensor.matmul(out, w_lo, x_hi, start=first, stop=False)
    nc.tensor.matmul(out, w_hi, x_lo, start=False, stop=False)
    return nc.tensor.matmul(out, w_hi, x_hi, start=False, stop=last)


CHUNK_TILES = 4
CHUNK = CHUNK_TILES * P


def feed_forward(nc, t, layer):
    three = layer == 0
    N = t.tiles // CHUNK_TILES
    steps = Steps(N, lead=2, lag=2, unroll=1)
    on = steps.on

    with ExitStack() as ctx:
        def sb(name, shape, dt=F32):
            return ctx.enter_context(nc.sbuf_tensor(f"f{name}{layer}", shape, dt))

        def psum(name, n=1):
            return ctx.enter_context(nc.psum_tensor(f"f{name}{layer}", [P, 512 * n], F32))

        def sem(name):
            return ctx.enter_context(nc.semaphore(f"f{name}{layer}"))

        stats = sb("stats", [P, CHUNK_TILES, 6])
        moments = sb("moments", [P, CHUNK_TILES, 2])
        spread = sb("spread", [P, CHUNK_TILES])
        rstd = sb("rstd", [P, CHUNK_TILES])
        normed = sb("normed", [P, CHUNK_TILES, P])
        x_hi, x_lo = sb("x_hi", [P, CHUNK], F32R), sb("x_lo", [P, CHUNK], F32R)
        LEVELS = 3 if three else 1
        h = sb("h", [P, 2, CHUNK])
        silu = sb("silu", [P, 2, CHUNK]) if three else None
        h_hi = [sb(f"h_hi{n}", [P, 4, CHUNK], F32R) for n in range(LEVELS)]
        h_lo = [sb(f"h_lo{n}", [P, 4, CHUNK], F32R) for n in range(LEVELS)]
        out_t = sb("out_t", [P, CHUNK])

        ps = psum("ps", 6)
        ps_in = psum("ps_in")
        ps_out = psum("ps_out")

        stats_chain = sem("stats_chain")
        spread_ready = sem("spread_ready")
        rstd_ready = sem("rstd_ready")
        norm_ready = sem("norm_ready")
        in_t_done = sem("in_t_done")
        x_hi_ready = sem("x_hi_ready")
        x_lo_ready = sem("x_lo_ready")
        done = [sem(f"done{n}") for n in range(LEVELS)]
        silu_ready = sem("silu_ready")
        act_ready = [sem(f"act_ready{n}") for n in range(LEVELS)]
        hi_ready = [sem(f"hi_ready{n}") for n in range(LEVELS)]
        lo_ready = [sem(f"lo_ready{n}") for n in range(LEVELS)]
        out_done = sem("out_done")
        out_taken = sem("out_taken")
        back_done = sem("back_done")
        x_done = sem("x_done")
        stored = sem("stored")

        def w(g):
            if three:
                return t.w_hi[:, g, :], t.w_lo[:, g, :]
            return t.f1_hi[:, g, :], t.f1_lo[:, g, :]

        def bank(n):
            return ps[:, n * 512:(n + 1) * 512]

        with nc.Block() as block:
            @block.tensor
            def _(pe):
                def turn_in(i):
                    if on(i):
                        wait(pe, norm_ready, i + 1)
                        wait(pe, x_lo_ready, i)
                        for k in range(CHUNK_TILES):
                            last = nc.tensor.transpose(ps_in[:, k * P:(k + 1) * P], normed[:, k, :], t.ident[:, :])
                        last.then_inc(in_t_done, 1)

                def up(i):
                    if not on(i):
                        return
                    wait(pe, x_lo_ready, i + 1)
                    if three:
                        wait(pe, act_ready[1], 4 * i)
                    for o in range(4):
                        cols = slice(o * P, (o + 1) * P)
                        if three:
                            if o == 3:
                                wait(pe, act_ready[0], 4 * i + 1)
                            pair = 2 * (o % 3)
                            for g in range(2):
                                hi, lo = w(g)
                                last = split_products(nc, bank(pair + g), hi[:, cols], lo[:, cols], x_hi[:, :], x_lo[:, :], True, True)
                        else:
                            wait(pe, act_ready[0], 4 * (i - 1) + o + 1)
                            hi, lo = w(0)
                            last = split_products(nc, bank(o), hi[:, cols], lo[:, cols], x_hi[:, :], x_lo[:, :], True, True)
                        last.then_inc(done[0], 1)

                def middle(i, level):
                    if not on(i):
                        return
                    wait(pe, lo_ready[level - 1], 4 * i + 4)
                    for o in range(4):
                        cols = slice(o * P, (o + 1) * P)
                        if level == 1:
                            wait(pe, act_ready[2], 4 * (i - 1) + o + 1)
                        else:
                            if isinstance(i, int) and i + 1 >= N:
                                wait(pe, act_ready[1], 4 * i + o + 1)
                            else:
                                wait(pe, act_ready[0], 4 * (i + 1) + (4 if o < 2 else 2))
                        for c in range(4):
                            hi, lo = w(2 + 4 * (level - 1) + c)
                            last = split_products(nc, bank(o), hi[:, cols], lo[:, cols],
                                                  h_hi[level - 1][:, c, :], h_lo[level - 1][:, c, :], c == 0, c == 3)
                        last.then_inc(done[level], 1)

                def down(i):
                    if not on(i):
                        return
                    wait(pe, lo_ready[LEVELS - 1], 4 * i + 4)
                    wait(pe, x_done, i)
                    hi, lo = w(10 if three else 1)
                    for c in range(4):
                        cols = slice(c * P, (c + 1) * P)
                        last = split_products(nc, ps_out[:, :], hi[:, cols], lo[:, cols],
                                              h_hi[LEVELS - 1][:, c, :], h_lo[LEVELS - 1][:, c, :], c == 0, c == 3)
                    last.then_inc(out_done, 1)

                def turn_back(i):
                    if on(i):
                        wait(pe, out_taken, i + 1)
                        for k in range(CHUNK_TILES):
                            last = nc.tensor.transpose(ps_out[:, k * P:(k + 1) * P], out_t[:, k * P:(k + 1) * P], t.ident[:, :])
                        last.then_inc(back_done, 1)

                def step(j, u):
                    turn_in(j + 1)
                    if three:
                        middle(j, 1)
                        down(j - 1)
                        up(j + 1)
                        turn_back(j - 1)
                        middle(j, 2)
                    else:
                        down(j - 1)
                        up(j)
                        turn_back(j - 1)

                steps.run(pe, step)

            @block.scalar
            def _(act):
                def hidden(i, level, func, scale=None, bias=None):
                    for o in range(4):
                        wait(act, done[level], 4 * i + o + 1)
                        wait(act, lo_ready[level], 4 * i + o - 1)
                        if o < 2 and level > 0:
                            if level == 1:
                                wait(act, lo_ready[2], 4 * i)
                            elif isinstance(i, int) and i + 1 >= N:
                                wait(act, lo_ready[1], 4 * i + 4)
                            else:
                                wait(act, lo_ready[0], 4 * i + 8)
                        nc.scalar.activation(h[:, o % 2, :], bank(o), func,
                                             scale=scale[:, o:o + 1] if scale is not None else 1.0,
                                             bias=bias[:, o:o + 1] if bias is not None else 0.0).then_inc(act_ready[level], 1)
                        split_hi(i, level, o)

                def split_hi(i, level, o):
                    wait(act, act_ready[level], 4 * i + o + 1)
                    wait(act, *readers(i, level))
                    nc.scalar.activation(h_hi[level][:, o, :], h[:, o % 2, :], ACT.Copy).then_inc(hi_ready[level], 1)

                def readers(i, level):
                    if level == LEVELS - 1:
                        return out_done, i
                    return done[level + 1], 4 * i

                def take_in(i):
                    if on(i):
                        wait(act, in_t_done, i + 1)
                        wait(act, done[0], 4 * i)
                        nc.scalar.activation(x_hi[:, :], ps_in[:, :], ACT.Copy).then_inc(x_hi_ready, 1)

                def take_out(i):
                    if on(i):
                        wait(act, out_done, i + 1)
                        wait(act, back_done, i)
                        if three:
                            nc.scalar.activation(out_t[:, :], ps_out[:, :], ACT.Copy, scale=t.s3[:, 0:1]).then_inc(out_taken, 1)
                        else:
                            nc.scalar.activation(out_t[:, :], ps_out[:, :], ACT.Identity, bias=t.b2[:, 0:1]).then_inc(out_taken, 1)

                def silu_stage(i):
                    if not on(i):
                        return
                    for o in range(4):
                        wait(act, done[0], 4 * i + o + 1)
                        wait(act, act_ready[0], 4 * i + o - 1)
                        nc.scalar.activation(silu[:, o % 2, :], bank(2 * (o % 3)), ACT.Silu,
                                             scale=t.s[:, 0, o:o + 1]).then_inc(silu_ready, 1)
                        if o > 0:
                            split_hi(i, 0, o - 1)
                    split_hi(i, 0, 3)

                def step(j, u):
                    take_in(j + 1)
                    if three:
                        if on(j):
                            hidden(j, 1, ACT.Gelu, scale=t.s[:, 2, :])
                        take_out(j - 1)
                        silu_stage(j + 1)
                        if on(j):
                            hidden(j, 2, ACT.Gelu, scale=t.s[:, 3, :])
                    else:
                        take_out(j - 1)
                        if on(j):
                            hidden(j, 0, ACT.Relu, bias=t.b1)

                steps.run(act, step)

            @block.gpsimd
            def _(pool):
                def step(j, u):
                    if on(j + 2):
                        wait(pool, spread_ready, j + 3)
                        wait(pool, norm_ready, j + 2)
                        nc.gpsimd.tensor_tensor(rstd[:, :], spread[:, :], t.minus_half[:, 0:CHUNK_TILES], ALU.pow).then_inc(rstd_ready, 1)

                steps.run(pool, step)

            @block.vector
            def _(dve):
                def split_lo(i, level, o):
                    wait(dve, hi_ready[level], 4 * i + o + 1)
                    nc.vector.tensor_tensor(h_lo[level][:, o, :], h[:, o % 2, :], h_hi[level][:, o, :].bitcast(F32),
                                            ALU.subtract).then_inc(lo_ready[level], 1)

                def measure(i):
                    for k in range(CHUNK_TILES):
                        last = nc.vector.bn_stats(stats[:, k, :], t.x[:, span(i * CHUNK_TILES + k, P)])
                    last.then_inc(stats_chain, 1)
                    wait(dve, stats_chain, 2 * i + 1)

                def moments_of(i):
                    for k in range(CHUNK_TILES):
                        last = nc.vector.bn_aggr(moments[:, k, :], stats[:, k, :])
                    last.then_inc(stats_chain, 1)
                    wait(dve, stats_chain, 2 * i + 2)
                    wait(dve, rstd_ready, i)
                    nc.vector.tensor_scalar(spread[:, :], moments[:, :, 1], EPS, None, ALU.add).then_inc(spread_ready, 1)

                def normalise(i):
                    if not on(i):
                        return
                    wait(dve, rstd_ready, i + 1)
                    wait(dve, in_t_done, i)
                    for k in range(CHUNK_TILES):
                        last = nc.vector.tensor_scalar(normed[:, k, :], t.x[:, span(i * CHUNK_TILES + k, P)], moments[:, k, 0:1],
                                                       rstd[:, k:k + 1], ALU.subtract, ALU.mult)
                    last.then_inc(norm_ready, 1)

                def split_in(i):
                    if on(i):
                        wait(dve, x_hi_ready, i + 1)
                        wait(dve, done[0], 4 * i)
                        nc.vector.tensor_tensor(x_lo[:, :], ps_in[:, :], x_hi[:, :].bitcast(F32), ALU.subtract).then_inc(x_lo_ready, 1)

                def product_stage(i):
                    if not on(i):
                        return
                    for o in range(4):
                        wait(dve, silu_ready, 4 * i + o + 1)
                        wait(dve, *((lo_ready[0], 4 * i + o - 1) if o > 1 else (lo_ready[1], 4 * i)))
                        nc.vector.scalar_tensor_tensor(out=h[:, o % 2, :], in0=bank(2 * (o % 3) + 1), scalar=t.s[:, 1, o:o + 1],
                                                       in1=silu[:, o % 2, :], op0=ALU.mult, op1=ALU.mult).then_inc(act_ready[0], 1)
                        if o > 0:
                            split_lo(i, 0, o - 1)
                    split_lo(i, 0, 3)

                def residual(i):
                    if on(i):
                        wait(dve, back_done, i + 1)
                        nc.vector.tensor_tensor(t.x[:, span(i, CHUNK)], ps_out[:, :], t.x[:, span(i, CHUNK)], ALU.add).then_inc(x_done, 1)

                def step(j, u):
                    split_in(j + 1)
                    if on(j + 2):
                        measure(j + 2)
                    if on(j):
                        split_lo(j, 1 if three else 0, 0)
                    if on(j + 2):
                        moments_of(j + 2)
                    if three:
                        if on(j):
                            for o in range(1, 4):
                                split_lo(j, 1, o)
                        product_stage(j + 1)
                        residual(j - 1)
                        normalise(j + 2)
                        if on(j):
                            for o in range(4):
                                split_lo(j, 2, o)
                    else:
                        if on(j):
                            for o in range(1, 4):
                                split_lo(j, 0, o)
                        normalise(j + 2)
                        residual(j - 1)

                steps.run(dve, step)

            @block.sync
            def _(sp):
                if three:
                    return
                xs = t.x[:, :].rearrange("p (t d) -> p t d", d=P)
                with sp.Fori(0, N) as i:
                    wait(sp, x_done, i + 1)
                    sp.dma_start(t.out.rearrange("(t b) s d -> (b s) t d", b=PER_TILE)[:, bass.ds(i * CHUNK_TILES, CHUNK_TILES), :],
                                 xs[:, bass.ds(i * CHUNK_TILES, CHUNK_TILES), :]).then_inc(stored, 16)
                sp.wait_ge(stored, 16 * N)


class Tensors:
    pass


def two_layer_xattn_ffn(nc, a, out):
    with ExitStack() as ctx:
        def sb(name, shape, dt=F32):
            return ctx.enter_context(nc.sbuf_tensor(name, shape, dt))

        t = Tensors()
        t.out = out
        t.tiles = a["x"].shape[0] // PER_TILE
        t.x = sb("x_res", [P, t.tiles * P])
        t.ctx = sb("ctx_res", [P, t.tiles * P])
        t.ident = sb("ident", [P, P])
        t.head_mask = sb("head_mask", [P, HEADS])
        t.ones_of_pair = sb("ones_of_pair", [P, 2, 32])
        t.minus_half = sb("minus_half", [P, 4])
        t.v_by_pair = sb("v_by_pair", [P, UNROLL, PER_TILE * PAIRS // 2, 96])
        t.wa = sb("wa", [P, 2, 4, P])
        t.qk_bias = sb("qk_bias", [P, 2, 2])
        t.bias_row = sb("bias_row", [P, 2, P])
        t.ln_o_g = sb("ln_o_g", [P, P])
        t.ln_o_b = sb("ln_o_b", [P, P])
        t.gate_w = sb("gate_w", [P, P])
        t.gate_nb = sb("gate_nb", [P, 1])
        t.w_hi = sb("w_hi", [P, 11, 512], F32R)
        t.w_lo = sb("w_lo", [P, 11, 512], F32R)
        t.f1_hi = sb("f1_hi", [P, 2, 512], F32R)
        t.f1_lo = sb("f1_lo", [P, 2, 512], F32R)
        t.s = sb("s", [P, 4, 4])
        t.s3 = sb("s3", [P, 1])
        t.b1 = sb("b1", [P, 4])
        t.b2 = sb("b2", [P, 1])

        prepare(nc, t, a)
        attention(nc, t, 0)
        feed_forward(nc, t, 0)
        attention(nc, t, 1)
        feed_forward(nc, t, 1)


def kernel(**inputs):
    import numpy as np
    import concourse.bacc as bacc
    from concourse.bass_utils import run_bass_kernel_spmd

    nc = bacc.Bacc("TRN2", target_bir_lowering=False, num_devices=1)
    arrays, args = {}, {}
    for name, value in inputs.items():
        array = np.ascontiguousarray(value)
        arrays[f"in_{name}"] = array
        args[name] = nc.dram_tensor(f"in_{name}", array.shape, mybir.dt.from_np(array.dtype), kind="ExternalInput").ap()
    x = inputs["x"]
    out = nc.dram_tensor("out_x", x.shape, F32, kind="ExternalOutput").ap()
    two_layer_xattn_ffn(nc, args, out)
    r = run_bass_kernel_spmd(nc, [arrays], core_ids=[0])
    return r.results[0]["out_x"]
```

```python
from contextlib import ExitStack

import concourse.bass as bass
from concourse import mybir

ALU = mybir.AluOpType
ACT = mybir.ActivationFunctionType
AX = mybir.AxisListType
F32 = mybir.dt.float32
F32R = mybir.dt.float32r
I32 = mybir.dt.int32

P = 128
EPS = 1e-5
HEADS = 16
HEAD_DIM = 8
SEQ = 64
PER_TILE = P // SEQ
PAIRS = HEADS // 2
PAIR_COLS = 32
UNROLL = 4


def wait(eng, sem, count):
    if isinstance(count, int) and count <= 0:
        return
    eng.wait_ge(sem, count)


def span(i, width):
    return slice(i * width, (i + 1) * width) if isinstance(i, int) else bass.ds(i * width, width)


class Steps:

    def __init__(self, total, lead, lag, unroll):
        self.total, self.first, self.last, self.unroll = total, -lead, total + lag, unroll
        self.lo = -(-lag // unroll) * unroll
        self.hi = (total - lead) // unroll * unroll

    def run(self, eng, step):
        for j in range(self.first, self.lo):
            step(j, j % self.unroll)
        with eng.Fori(self.lo, self.hi, self.unroll) as base:
            for u in range(self.unroll):
                step(base + u, u)
        for j in range(self.hi, self.last):
            step(j, j % self.unroll)

    def on(self, i):
        return not isinstance(i, int) or 0 <= i < self.total


def column(a):
    return a.rearrange("(p a) -> p a", a=1)


def row_everywhere(a):
    return a.rearrange("(a n) -> a n", a=1).to_broadcast([P, P])


def prepare(nc, t, a):
    with ExitStack() as ctx:
        def sb(name, shape, dt=F32):
            return ctx.enter_context(nc.sbuf_tensor(name, shape, dt))

        def sem(name):
            return ctx.enter_context(nc.semaphore(name))

        raw = sb("raw_ffn0", [P, 11, 4, P])
        raw_l1 = sb("raw_l1", [P, 4, P])
        raw_l0 = sb("raw_l0", [P, 4, P])
        raw_w1 = sb("raw_w1", [P, 4, P])
        raw_w2 = sb("raw_w2", [P, 4, P])
        cols = sb("cols", [P, 11])
        rows = sb("rows", [P, 2, P])
        sums = sb("sums", [P, 4])
        vb = sb("vb", [P, 2])
        lo_top = sb("lo_top", [P, 1])
        vb_wide = sb("vb_wide", [P, 2, P])
        ps = ctx.enter_context(nc.psum_tensor("prep_ps", [P, 4, 512], F32))
        ps_b = ctx.enter_context(nc.psum_tensor("prep_ps_b", [P, 512], F32))
        ps_r = ctx.enter_context(nc.psum_tensor("prep_ps_r", [P, 2, 512], F32))

        ld_small, ld_l, ld_x, ld_c = sem("ld_small"), sem("ld_l"), sem("ld_x"), sem("ld_c")
        ld_raw = [sem(f"ld_raw{g}") for g in range(5)]
        ld_w = sem("ld_w")
        ident_zero, ident_ready, consts_ready = sem("ident_zero"), sem("ident_ready"), sem("consts_ready")
        v_zero = sem("v_zero")
        turned = sem("turned")
        hi_taken, lo_taken = sem("hi_taken"), sem("lo_taken")
        l1_taken = sem("l1_taken")
        lo_top_ready, lo_row_ready = sem("lo_top_ready"), sem("lo_row_ready")
        bias_ps, bias_row_ps = sem("bias_ps"), sem("bias_row_ps")
        vb_ready = sem("vb_ready")
        chain = sem("prep_chain")
        scaled = sem("prep_scaled")

        XQ = 4
        NT = t.tiles // XQ
        GROUPS = [("w1", 0), ("w2", 0)] + [("h1", c) for c in range(4)] + [("h2", c) for c in range(4)] + [("w3", 0)]

        with nc.Block() as block:
            @block.sync
            def _(sp):
                sp.dma_start(raw_l0[:, 0, :], a["L0_xattn_Wq"]).then_inc(ld_l, 16)
                sp.dma_start(raw_l0[:, 1, :], a["L0_xattn_Wk"]).then_inc(ld_l, 16)
                sp.dma_start(raw_l0[:, 2, :], a["L0_xattn_Wv"]).then_inc(ld_l, 16)
                sp.dma_start(raw_l0[:, 3, :], a["L0_xattn_Wo"]).then_inc(ld_l, 16)
                for n, k in enumerate(("w_q", "w_k", "w_v", "w_o")):
                    sp.dma_start(raw_l1[:, n, :], a[f"L1_xattn_{k}"]).then_inc(ld_l, 16)
                xv = a["x"].rearrange("(t b) s d -> (b s) t d", b=PER_TILE)
                cv = a["ctx_1024"].rearrange("(t b) s d -> (b s) t d", b=PER_TILE)
                xs = t.x[:, :].rearrange("p (t d) -> p t d", d=P)
                cs = t.ctx[:, :].rearrange("p (t d) -> p t d", d=P)
                for n in range(XQ):
                    sp.dma_start(xs[:, n * NT:(n + 1) * NT, :], xv[:, n * NT:(n + 1) * NT, :]).then_inc(ld_x, 16)
                    sp.dma_start(cs[:, n * NT:(n + 1) * NT, :], cv[:, n * NT:(n + 1) * NT, :]).then_inc(ld_c, 16)
                sp.wait_ge(ld_x, 16 * XQ)
                sp.wait_ge(ld_c, 16 * XQ)

            @block.scalar
            def _(act):
                names = ["L0_xattn_bq", "L0_xattn_bk", "L0_xattn_bv", "L0_xattn_ln_q_g", "L0_xattn_ln_q_b",
                         "L0_xattn_ln_kv_g", "L0_xattn_ln_kv_b", "L1_xattn_b_q", "L1_xattn_b_k", "L1_xattn_b_v"]
                for n, k in enumerate(names):
                    act.dma_start(cols[:, n:n + 1], column(a[k])).then_inc(ld_small, 16)
                act.dma_start(cols[:, 10:11], a["L0_xattn_Wg"]).then_inc(ld_small, 16)
                act.dma_start(rows[:, 0, :], row_everywhere(a["L0_xattn_Wg"].rearrange("d a -> (d a)"))).then_inc(ld_small, 16)
                act.dma_start(rows[:, 1, :], row_everywhere(a["L0_xattn_ln_q_b"])).then_inc(ld_small, 16)
                act.dma_start(t.bias_row[:, 0, :], row_everywhere(a["L0_xattn_bo"])).then_inc(ld_small, 16)
                act.dma_start(t.bias_row[:, 1, :], row_everywhere(a["L1_xattn_b_o"])).then_inc(ld_small, 16)
                act.dma_start(t.ln_o_g[:, :], row_everywhere(a["L0_xattn_ln_o_g"])).then_inc(ld_small, 16)
                act.dma_start(t.ln_o_b[:, :], row_everywhere(a["L0_xattn_ln_o_b"])).then_inc(ld_small, 16)
                for n, k in enumerate(("w1_s", "w2_s", "h1_s", "h2_s")):
                    act.dma_start(t.s[:, n, :], a[f"L0_ffn_{k}"].rearrange("(o p) -> p o", p=P),
                                  allow_slow_non_contiguous=True).then_inc(ld_small, 16)
                act.dma_start(t.s3[:, :], column(a["L0_ffn_w3_s"])).then_inc(ld_small, 16)
                act.dma_start(t.b1[:, :], a["L1_ffn_b1"].rearrange("(o p) -> p o", p=P),
                              allow_slow_non_contiguous=True).then_inc(ld_small, 16)
                act.dma_start(t.b2[:, :], column(a["L1_ffn_b2"])).then_inc(ld_small, 16)
                for g in range(11):
                    act.wait_ge(turned, g + 1)
                    act.activation(t.w_hi[:, g, :], ps[:, g % 4, :], ACT.Copy).then_inc(hi_taken, 1)
                act.wait_ge(turned, 12)
                for n in (0, 1, 3):
                    act.activation(t.wa[:, 1, n, :], ps[:, 3, n * P:(n + 1) * P], ACT.Copy)
                act.activation(t.wa[:, 1, 2, :].rearrange("p (q c d) -> p q c d", q=2, d=HEAD_DIM),
                               ps[:, 3, 2 * P:3 * P].rearrange("p (c q d) -> p q c d", q=2, d=HEAD_DIM), ACT.Copy).then_inc(l1_taken, 1)
                act.wait_ge(ld_w, 32)
                act.activation(t.f1_hi[:, 0, :], raw_w1[:, :, :], ACT.Copy)
                act.activation(t.f1_hi[:, 1, :], raw_w2[:, :, :], ACT.Copy).then_inc(hi_taken, 1)

            @block.gpsimd
            def _(pool):
                pool.dma_start(raw[:, 0, :, :], a["L0_ffn_w1_w"].rearrange("(r p) i -> p r i", p=P)).then_inc(ld_raw[0], 16)
                pool.dma_start(raw[:, 1, :, :], a["L0_ffn_w2_w"].rearrange("(r p) i -> p r i", p=P)).then_inc(ld_raw[1], 16)
                for g0, k, s in ((2, "h1_w", 2), (6, "h2_w", 3)):
                    for c in range(4):
                        pool.dma_start(raw[:, g0 + c, :, :], a[f"L0_ffn_{k}"][:, c * P:(c + 1) * P]
                                       .rearrange("(r p) i -> p r i", p=P)).then_inc(ld_raw[s], 16)
                pool.dma_start(raw[:, 10, :, :], a["L0_ffn_w3_w"].rearrange("p (c i) -> p c i", i=P)).then_inc(ld_raw[4], 16)
                pool.dma_start(raw_w1[:, :, :], a["L1_ffn_W1"].rearrange("p (o i) -> p o i", i=P)).then_inc(ld_w, 16)
                pool.dma_start(raw_w2[:, :, :], a["L1_ffn_W2"].rearrange("(c p) o -> p c o", p=P)).then_inc(ld_w, 16)
                nc.gpsimd.memset(t.ident[:, :], 0.0).then_inc(ident_zero, 1)
                nc.gpsimd.memset(t.head_mask[:, :], 1.0).then_inc(ident_zero, 1)
                nc.gpsimd.memset(t.minus_half[:, :], -0.5)
                nc.gpsimd.memset(t.v_by_pair[:, :, :, :], 0.0).then_inc(v_zero, 1)
                pool.wait_ge(ident_zero, 2)
                nc.gpsimd.affine_select(out=t.ident[:, :], in_=t.ident[:, :], compare_op=ALU.not_equal, fill=1.0,
                                        base=0, pattern=[[-1, P]], channel_multiplier=1).then_inc(ident_ready, 1)
                nc.gpsimd.affine_select(out=t.head_mask[:, :], in_=t.head_mask[:, :], compare_op=ALU.is_ge, fill=0.0,
                                        base=0, pattern=[[-HEAD_DIM, HEADS]], channel_multiplier=1).then_inc(consts_ready, 1)
                pool.wait_ge(consts_ready, 1)
                nc.gpsimd.affine_select(out=t.head_mask[:, :], in_=t.head_mask[:, :], compare_op=ALU.is_ge, fill=0.0,
                                        base=HEAD_DIM - 1, pattern=[[HEAD_DIM, HEADS]], channel_multiplier=-1).then_inc(consts_ready, 1)

            @block.tensor
            def _(pe):
                pe.wait_ge(ld_l, 128)
                pe.wait_ge(ld_small, 16 * 24)
                nc.tensor.matmul(ps_b[:, 0:1], raw_l0[:, 0, :], cols[:, 4:5], start=True, stop=True)
                nc.tensor.matmul(ps_b[:, 1:2], raw_l0[:, 1, :], cols[:, 6:7], start=True, stop=True)
                nc.tensor.matmul(ps_b[:, 2:3], raw_l0[:, 2, :], cols[:, 6:7], start=True, stop=True).then_inc(bias_ps, 1)
                pe.wait_ge(ident_ready, 1)
                for g in range(11):
                    which = g if g < 2 else 2 if g < 6 else 3 if g < 10 else 4
                    pe.wait_ge(ld_raw[which], 64 if which in (2, 3) else 16)
                    if g >= 4:
                        pe.wait_ge(hi_taken, g - 3)
                        pe.wait_ge(lo_taken, g - 3)
                    for r in range(4):
                        last = nc.tensor.transpose(ps[:, g % 4, r * P:(r + 1) * P], raw[:, g, r, :], t.ident[:, :])
                    last.then_inc(turned, 1)
                pe.wait_ge(hi_taken, 8)
                pe.wait_ge(lo_taken, 8)
                for r in range(4):
                    last = nc.tensor.transpose(ps[:, 3, r * P:(r + 1) * P], raw_l1[:, r, :], t.ident[:, :])
                last.then_inc(turned, 1)
                pe.wait_ge(lo_top_ready, 1)
                nc.tensor.transpose(ps_b[0:1, P:2 * P], lo_top[:, 0:1], t.ident[:, :]).then_inc(lo_row_ready, 1)
                pe.wait_ge(vb_ready, 1)
                nc.tensor.matmul(ps_r[:, 0, 0:P], vb_wide[:, 0, :], raw_l0[:, 3, :], start=True, stop=True)
                pe.wait_ge(l1_taken, 1)
                nc.tensor.matmul(ps_r[:, 1, 0:P], vb_wide[:, 1, :], t.wa[:, 1, 3, :], start=True, stop=True).then_inc(bias_row_ps, 1)

            @block.vector
            def _(dve):
                s = float(HEAD_DIM) ** -0.5
                dve.wait_ge(v_zero, 1)
                for h2 in range(2):
                    c0 = 2 * HEAD_DIM + h2
                    nc.vector.memset(t.v_by_pair[h2 * SEQ:(h2 + 1) * SEQ, :, :, c0:c0 + 1], 1.0)
                dve.wait_ge(ld_l, 128)
                dve.wait_ge(ld_small, 16 * 24)
                nc.vector.tensor_scalar(t.wa[:, 0, 0, :], raw_l0[:, 0, :], cols[:, 3:4], s, ALU.mult, ALU.mult)
                nc.vector.tensor_scalar(t.wa[:, 0, 1, :], raw_l0[:, 1, :], cols[:, 5:6], None, ALU.mult)
                by_half = "p (q c d) -> p q c d", "p (c q d) -> p q c d"
                nc.vector.tensor_scalar(t.wa[:, 0, 2, :].rearrange(by_half[0], q=2, d=HEAD_DIM),
                                        raw_l0[:, 2, :].rearrange(by_half[1], q=2, d=HEAD_DIM), cols[:, 5:6], None, ALU.mult)
                nc.vector.tensor_copy(t.wa[:, 0, 3, :], raw_l0[:, 3, :])
                nc.vector.tensor_tensor(t.gate_w[:, :], cols[:, 10:11], cols[:, 3:4], ALU.mult)
                nc.vector.tensor_tensor_reduce(out=vb_wide[:, 0, :], in0=rows[:, 0, :], in1=rows[:, 1, :], scale=1.0, scalar=0.0,
                                               op0=ALU.mult, op1=ALU.add, accum_out=sums[:, 0:1]).then_inc(chain, 1)
                dve.wait_ge(chain, 1)
                nc.vector.tensor_scalar(t.gate_nb[:, :], sums[:, 0:1], -1.0, None, ALU.mult)
                dve.wait_ge(bias_ps, 1)
                nc.vector.tensor_tensor(sums[:, 1:2], ps_b[:, 0:1], cols[:, 0:1], ALU.add)
                nc.vector.tensor_tensor(t.qk_bias[:, 0, 1:2], ps_b[:, 1:2], cols[:, 1:2], ALU.add)
                nc.vector.tensor_tensor(vb[:, 0:1], ps_b[:, 2:3], cols[:, 2:3], ALU.add)
                nc.vector.tensor_copy(vb[:, 1:2], cols[:, 9:10])
                nc.vector.tensor_scalar(t.qk_bias[:, 1, 0:1], cols[:, 7:8], s, None, ALU.mult)
                nc.vector.tensor_copy(t.qk_bias[:, 1, 1:2], cols[:, 8:9]).then_inc(chain, 1)
                dve.wait_ge(chain, 2)
                nc.vector.tensor_scalar(t.qk_bias[:, 0, 0:1], sums[:, 1:2], s, None, ALU.mult)
                nc.vector.tensor_copy(vb_wide[:, :, :], vb[:, :].unsqueeze(2).to_broadcast([P, 2, P])).then_inc(vb_ready, 1)
                for g in range(11):
                    dve.wait_ge(hi_taken, g + 1)
                    nc.vector.tensor_tensor(t.w_lo[:, g, :], ps[:, g % 4, :], t.w_hi[:, g, :].bitcast(F32), ALU.subtract).then_inc(lo_taken, 1)
                dve.wait_ge(lo_taken, 11)
                dve.wait_ge(hi_taken, 12)
                nc.vector.tensor_tensor(t.f1_lo[:, 0, :], raw_w1[:, :, :].rearrange("p o i -> p (o i)"),
                                        t.f1_hi[:, 0, :].bitcast(F32), ALU.subtract)
                nc.vector.tensor_tensor(t.f1_lo[:, 1, :], raw_w2[:, :, :].rearrange("p o i -> p (o i)"),
                                        t.f1_hi[:, 1, :].bitcast(F32), ALU.subtract)
                nc.vector.tensor_reduce(out=lo_top[:, 0:1], in_=t.w_lo[:, :, :].rearrange("p g n -> p (g n)").bitcast(F32),
                                        op=ALU.max, axis=AX.X, apply_absolute_value=True).then_inc(lo_top_ready, 1)
                dve.wait_ge(lo_row_ready, 1)
                nc.vector.tensor_reduce(out=t.lo_bits[0:1, 0:1], in_=ps_b[0:1, P:2 * P], op=ALU.max, axis=AX.X)
                dve.wait_ge(bias_row_ps, 1)
                nc.vector.tensor_tensor(t.bias_row[:, 0, :], t.bias_row[:, 0, :], ps_r[:, 0, 0:P], ALU.add)
                nc.vector.tensor_tensor(t.bias_row[:, 1, :], t.bias_row[:, 1, :], ps_r[:, 1, 0:P], ALU.add)
                nc.vector.tensor_scalar(t.wa[:, 1, 0, :], t.wa[:, 1, 0, :], s, None, ALU.mult)


def attention(nc, t, layer):
    gated = layer == 0
    T = t.tiles
    steps = Steps(T, lead=5, lag=9, unroll=UNROLL)
    on = steps.on
    wq, wk, wv, wo = (t.wa[:, layer, n, :] for n in range(4))

    with ExitStack() as ctx:
        def sb(name, shape, dt=F32):
            return ctx.enter_context(nc.sbuf_tensor(f"{name}{layer}", shape, dt))

        def psum(name, n=1):
            return ctx.enter_context(nc.psum_tensor(f"{name}{layer}", [P, 512 * n], F32))

        def sem(name):
            return ctx.enter_context(nc.semaphore(f"{name}{layer}"))

        stats = sb("stats", [P, UNROLL, 2, 6])
        moments = sb("moments", [P, UNROLL, 2, 2])
        spread = sb("spread", [P, UNROLL, 3])
        rstd = sb("rstd", [P, UNROLL, 3])
        offset = sb("offset", [P, UNROLL, 2])
        normed = sb("normed", [P, UNROLL, 2, P])
        turned = sb("turned", [P, 2, 2, P])
        q_t = sb("q_t", [P, UNROLL, P])
        k_t = sb("k_t", [P, UNROLL, P])
        k_heads = sb("k_heads", [P, 2, HEADS, P])
        top = sb("top", [P, 2, HEADS])
        prob = sb("prob", [P, 2, HEADS * SEQ])
        prob_t = sb("prob_t", [P, 2, PAIRS, P])
        sums_t = sb("sums_t", [P, 2, 2, P])
        rden = sb("rden", [P, 2, PAIRS, 2])
        heads_out = sb("heads_out", [P, 2, P])
        out_t = sb("out_t", [P, 2, P])
        if gated:
            gate_exp = sb("gate_exp", [P, T])
            gate = sb("gate", [P, UNROLL])
            y = sb("y", [P, UNROLL, P])
            y_stats = sb("y_stats", [P, 6])
            y_moments = sb("y_moments", [P, UNROLL, 2])
            y_tmp = sb("y_tmp", [P, UNROLL])
            y_scale = sb("y_scale", [P, 1])
            y_gain = sb("y_gain", [P, P])

        ps_s = psum("ps_s", 2)
        ps_pt = psum("ps_pt", 2)
        ps_in = psum("ps_in")
        ps_qkv = psum("ps_qkv")
        ps_o = psum("ps_o")
        ps_y = psum("ps_y")

        ln_chain = sem("ln_chain")
        spread_ready = sem("spread_ready")
        rstd_ready = sem("rstd_ready")
        offset_ready = sem("offset_ready")
        norm_ready = sem("norm_ready")
        in_t_done = sem("in_t_done")
        in_t_taken = sem("in_t_taken")
        qkv_done = sem("qkv_done")
        k_taken = sem("k_taken")
        qkv_taken = sem("qkv_taken")
        k_heads_ready = sem("k_heads_ready")
        scores_done = sem("scores_done")
        top_ready = sem("top_ready")
        shifted = sem("shifted")
        exp_done = sem("exp_done")
        prob_t_done = sem("prob_t_done")
        prob_t_taken = sem("prob_t_taken")
        pv_done = sem("pv_done")
        sums_taken = sem("sums_taken")
        sums_back = sem("sums_back")
        rden_ready = sem("rden_ready")
        heads_ready = sem("heads_ready")
        heads_t_done = sem("heads_t_done")
        out_t_ready = sem("out_t_ready")
        y_done = sem("y_done")
        y_taken = sem("y_taken")
        biased = sem("biased")
        y_chain = sem("y_chain")
        y_spread_ready = sem("y_spread_ready")
        y2_chain = sem("y2_chain")
        x_done = sem("x_done")

        closing_row = t.ln_o_b[:, :] if gated else t.bias_row[:, 1, :]
        NORMS = 2 if gated else 1

        def upto(count):
            return min(count, T) if isinstance(count, int) else count

        def rstd_step(j):
            return j + 6

        with nc.Block() as block:
            @block.tensor
            def _(pe):
                def step(j, u):
                    if on(j):
                        wait(pe, qkv_taken, j + 1)
                        wait(pe, k_heads_ready, j + 1)
                        wait(pe, shifted, j)
                        for half in range(2):
                            for b in range(PER_TILE):
                                last = nc.tensor.matmul(
                                    ps_s[b * SEQ:(b + 1) * SEQ, half * 512:(half + 1) * 512],
                                    q_t[:, u, b * SEQ:(b + 1) * SEQ],
                                    k_heads[:, u % 2, half * 8:(half + 1) * 8, b * SEQ:(b + 1) * SEQ],
                                    start=True, stop=True)
                        last.then_inc(scores_done, 1)
                    i, s = j - 5, (u - 5) % UNROLL
                    if on(i):
                        wait(pe, out_t_ready, i + 1)
                        wait(pe, y_taken, i)
                        nc.tensor.matmul(ps_y[:, 0:P], out_t[:, s % 2, :], wo, start=True, stop=True).then_inc(y_done, 1)
                    i, s = j - 3, (u - 3) % UNROLL
                    if on(i):
                        wait(pe, sums_taken, i + 1)
                        wait(pe, heads_ready, i)
                        wait(pe, in_t_taken, upto(j + 3))
                        for half in range(2):
                            last = nc.tensor.transpose(ps_in[:, (2 + half) * P:(3 + half) * P], sums_t[:, s % 2, half, :], t.ident[:, :])
                        last.then_inc(sums_back, 1)
                    i, s = j + 3, (u + 3) % UNROLL
                    if on(i):
                        wait(pe, norm_ready, i + 1)
                        wait(pe, in_t_taken, i)
                        wait(pe, heads_ready, j - 3)
                        for n in range(2):
                            last = nc.tensor.transpose(ps_in[:, n * P:(n + 1) * P], normed[:, s, n, :], t.ident[:, :])
                        last.then_inc(in_t_done, 1)
                    i, s = j - 4, u
                    if on(i):
                        wait(pe, heads_ready, i + 1)
                        wait(pe, out_t_ready, i)
                        wait(pe, sums_taken, upto(j - 2))
                        nc.tensor.transpose(ps_o[:, 2 * P:3 * P], heads_out[:, s % 2, :], t.ident[:, :]).then_inc(heads_t_done, 1)
                    i, s = j - 2, (u - 2) % UNROLL
                    if on(i):
                        wait(pe, prob_t_taken, i + 1)
                        wait(pe, sums_taken, i)
                        for b in range(PER_TILE):
                            for half in range(2):
                                for c in range(4):
                                    hp = 4 * half + c
                                    last = nc.tensor.matmul(
                                        ps_o[PAIR_COLS * c:PAIR_COLS * (c + 1), half * P + b * SEQ:half * P + (b + 1) * SEQ],
                                        t.v_by_pair[:, s, b * PAIRS + hp, :],
                                        prob_t[:, s % 2, hp, b * SEQ:(b + 1) * SEQ], start=True, stop=True)
                        last.then_inc(pv_done, 1)
                    i, s = j - 1, (u - 1) % UNROLL
                    if on(i):
                        wait(pe, exp_done, i + 1)
                        wait(pe, prob_t_taken, i)
                        for hp in range(PAIRS):
                            last = nc.tensor.transpose(ps_pt[:, hp * P:(hp + 1) * P],
                                                       prob[:, s % 2, hp * P:(hp + 1) * P], t.ident[:, :])
                        last.then_inc(prob_t_done, 1)
                    i, s = j + 2, (u + 2) % UNROLL
                    if on(i):
                        wait(pe, in_t_taken, i + 1)
                        wait(pe, qkv_taken, i)
                        nc.tensor.matmul(ps_qkv[:, P:2 * P], wk, turned[:, s % 2, 1, :], start=True, stop=True)
                        nc.tensor.matmul(ps_qkv[:, 0:P], wq, turned[:, s % 2, 0, :], start=True, stop=True)
                        for b in range(PER_TILE):
                            for h2 in range(2):
                                last = nc.tensor.matmul(
                                    ps_qkv[h2 * SEQ:(h2 + 1) * SEQ, 2 * P + b * SEQ:2 * P + (b + 1) * SEQ],
                                    turned[:, s % 2, 1, b * SEQ:(b + 1) * SEQ],
                                    wv[:, h2 * SEQ:(h2 + 1) * SEQ], start=True, stop=True)
                        if gated:
                            last = nc.tensor.matmul(ps_qkv[:, 3 * P:3 * P + 1], turned[:, s % 2, 0, :], t.gate_w[:, :], start=True, stop=True)
                        last.then_inc(qkv_done, 1)
                steps.run(pe, step)

            @block.scalar
            def _(act):
                def step(j, u):
                    i, s = j + 3, (u + 3) % UNROLL
                    if on(i):
                        wait(act, in_t_done, i + 1)
                        wait(act, qkv_done, i - 1)
                        nc.scalar.activation(turned[:, s % 2, :, :], ps_in[:, 0:2 * P].rearrange("p (n d) -> p n d", n=2),
                                             ACT.Copy).then_inc(in_t_taken, 1)
                    i, s = j - 4, u
                    if on(i):
                        wait(act, heads_t_done, i + 1)
                        wait(act, pv_done, upto(j - 1))
                        wait(act, y_done, i - 1)
                        nc.scalar.activation(out_t[:, s % 2, :], ps_o[:, 2 * P:3 * P], ACT.Copy).then_inc(out_t_ready, 1)
                    i, s = j - 2, (u - 2) % UNROLL
                    if on(i):
                        wait(act, pv_done, i + 1)
                        wait(act, sums_back, i - 1)
                        nc.scalar.activation(sums_t[:, s % 2, :, :], ps_o[:, 0:2 * P].rearrange("p (n d) -> p n d", n=2),
                                             ACT.Copy).then_inc(sums_taken, 1)

                    i, s = j - 1, (u - 1) % UNROLL
                    if on(i):
                        wait(act, prob_t_done, i + 1)
                        wait(act, pv_done, i - 1)
                        nc.scalar.activation(prob_t[:, s % 2, :, :], ps_pt[:, :].rearrange("p (n d) -> p n d", n=PAIRS),
                                             ACT.Copy).then_inc(prob_t_taken, 1)
                    i, s = j + 2, (u + 2) % UNROLL
                    if on(i):
                        wait(act, qkv_done, i + 1)
                        wait(act, k_heads_ready, i - 3)
                        nc.scalar.activation(k_t[:, s, :], ps_qkv[:, P:2 * P], ACT.Identity,
                                             bias=t.qk_bias[:, layer, 1:2]).then_inc(k_taken, 1)
                        wait(act, scores_done, i - 3)
                        nc.scalar.activation(q_t[:, s, :], ps_qkv[:, 0:P], ACT.Identity,
                                             bias=t.qk_bias[:, layer, 0:1], scale=1.0)
                        wait(act, pv_done, i - 3)
                        for h2 in range(2):
                            rows = slice(h2 * SEQ, (h2 + 1) * SEQ)
                            last = nc.scalar.activation(
                                t.v_by_pair[rows, s, :, h2 * HEAD_DIM:(h2 + 1) * HEAD_DIM],
                                ps_qkv[rows, 2 * P:3 * P].rearrange("p (m d) -> p m d", d=HEAD_DIM), ACT.Copy)
                        if gated:
                            last = nc.scalar.activation(gate_exp[:, span(i, 1)], ps_qkv[:, 3 * P:3 * P + 1], ACT.Exp, scale=-1.0,
                                                        bias=t.gate_nb[:, 0:1])
                        last.then_inc(qkv_taken, 1)
                    i, s = j + 4, u
                    if on(i):
                        wait(act, offset_ready, i + 1)
                        wait(act, in_t_done, i - 3)
                        src = (t.x[:, span(i, P)], t.ctx[:, span(i, P)])
                        for k in range(NORMS):
                            last = nc.scalar.activation(normed[:, s, k, :], src[k], ACT.Identity,
                                                        scale=rstd[:, s, k:k + 1], bias=offset[:, s, k:k + 1])
                        if not gated:
                            last = nc.scalar.activation(normed[:, s, 1, :], src[1], ACT.Copy)
                        last.then_inc(norm_ready, 1)
                    if on(j):
                        wait(act, shifted, j + 1)
                        nc.scalar.activation(prob[:, u % 2, :], prob[:, u % 2, :], ACT.Exp).then_inc(exp_done, 1)
                steps.run(act, step)

            @block.gpsimd
            def _(pool):
                def step(j, u):
                    i, s = j + 1, (u + 1) % UNROLL
                    if on(i):
                        wait(pool, k_taken, i + 1)
                        wait(pool, scores_done, i - 1)
                        nc.gpsimd.tensor_tensor(k_heads[:, s % 2, :, :],
                                                k_t[:, s, :].unsqueeze(1).to_broadcast([P, HEADS, P]),
                                                t.head_mask[:, :].unsqueeze(2).to_broadcast([P, HEADS, P]),
                                                ALU.mult).then_inc(k_heads_ready, 1)
                    i, s = j + 5, (u + 5) % UNROLL
                    first, last = NORMS, 0
                    if on(i):
                        wait(pool, spread_ready, i + 1)
                        wait(pool, norm_ready, i - 3)
                        first, last = 0, NORMS
                    if gated and on(j - 7):
                        wait(pool, y_spread_ready, j - 6)
                        wait(pool, x_done, j - 10)
                        last = 3
                    if last:
                        nc.gpsimd.tensor_tensor(rstd[:, s, first:last], spread[:, s, first:last], t.minus_half[:, first:last],
                                                ALU.pow).then_inc(rstd_ready, 1)
                    if on(j):
                        wait(pool, norm_ready, j + 1)
                        nc.gpsimd.tensor_tensor(t.x[:, span(j, P)], t.x[:, span(j, P)], closing_row, ALU.add).then_inc(biased, 1)

                steps.run(pool, step)

            @block.vector
            def _(dve):
                def step(j, u):
                    k, f = j, j + 5
                    b, sb_ = j - 6, (u - 6) % UNROLL
                    c, sc = j - 4, u
                    a, sa = j - 8, u
                    sf = (u + 5) % UNROLL
                    sums = ps_in[:, 2 * P:4 * P].rearrange("p (m r) -> p m r", r=PAIR_COLS)
                    if gated and on(b):
                        wait(dve, y_done, b + 1)
                        wait(dve, x_done, b - 3)
                        nc.vector.tensor_tensor(y[:, sb_, :], ps_y[:, 0:P], t.bias_row[:, 0, :], ALU.add).then_inc(y_taken, 1)
                    if not gated and on(b):
                        wait(dve, y_done, b + 1)
                        wait(dve, biased, b + 1)
                        nc.vector.tensor_tensor(t.x[:, span(b, P)], ps_y[:, 0:P], t.x[:, span(b, P)], ALU.add).then_inc(y_taken, 1)
                    if on(c):
                        wait(dve, sums_back, c + 1)
                        wait(dve, in_t_taken, upto(j + 3))
                        nc.vector.reciprocal(rden[:, sc % 2, :, :], sums[:, :, 2 * HEAD_DIM:2 * HEAD_DIM + 2]).then_inc(rden_ready, 1)
                    if gated and on(b):
                        nc.vector.tensor_scalar(gate[:, sb_:sb_ + 1], gate_exp[:, span(b, 1)], 1.0, None, ALU.add).then_inc(y_chain, 1)
                        wait(dve, y_taken, b + 1)
                        nc.vector.bn_stats(y_stats[:, :], y[:, sb_, :]).then_inc(y_chain, 1)
                    if on(c):
                        wait(dve, rden_ready, c + 1)
                        wait(dve, heads_t_done, c - 1)
                        nc.vector.tensor_tensor(heads_out[:, sc % 2, :].rearrange("p (m h d) -> p m h d", h=2, d=HEAD_DIM),
                                                sums[:, :, 0:2 * HEAD_DIM].rearrange("p m (h d) -> p m h d", d=HEAD_DIM),
                                                rden[:, sc % 2, :, :].unsqueeze(3).to_broadcast([P, PAIRS, 2, HEAD_DIM]),
                                                ALU.mult).then_inc(heads_ready, 1)
                    if gated and on(b):
                        wait(dve, y_chain, 5 * b + 2)
                        nc.vector.reciprocal(gate[:, sb_:sb_ + 1], gate[:, sb_:sb_ + 1]).then_inc(y_chain, 1)
                        nc.vector.bn_aggr(y_moments[:, sb_, :], y_stats[:, :]).then_inc(y_chain, 1)
                    if gated and on(a):
                        wait(dve, rstd_ready, rstd_step(j - 1))
                        wait(dve, x_done, a)
                        nc.vector.tensor_tensor(y_scale[:, 0:1], rstd[:, sa, 2:3], gate[:, sa:sa + 1], ALU.mult)
                        nc.vector.scalar_tensor_tensor(out=y_gain[:, :], in0=y[:, sa, :], scalar=y_moments[:, sa, 0:1],
                                                       in1=t.ln_o_g[:, :], op0=ALU.subtract, op1=ALU.mult).then_inc(y2_chain, 1)
                    if gated and on(b):
                        wait(dve, y_chain, 5 * b + 4)
                        nc.vector.tensor_scalar(y_tmp[:, sb_:sb_ + 1], y_moments[:, sb_, 1:2], gate[:, sb_:sb_ + 1], gate[:, sb_:sb_ + 1],
                                                ALU.mult, ALU.mult).then_inc(y_chain, 1)
                    if on(f):
                        src = (t.x[:, span(f, P)], t.ctx[:, span(f, P)])
                        for n in range(NORMS):
                            last = nc.vector.bn_stats(stats[:, sf, n, :], src[n])
                        last.then_inc(ln_chain, 1)
                    if gated and on(a):
                        wait(dve, y2_chain, a + 1)
                        wait(dve, biased, a + 1)
                        nc.vector.scalar_tensor_tensor(out=t.x[:, span(a, P)], in0=y_gain[:, :], scalar=y_scale[:, 0:1],
                                                       in1=t.x[:, span(a, P)], op0=ALU.mult, op1=ALU.add).then_inc(x_done, 1)
                    if gated and on(b):
                        wait(dve, y_chain, 5 * b + 5)
                        wait(dve, rstd_ready, rstd_step(j - 3))
                        nc.vector.tensor_scalar(spread[:, sb_, 2:3], y_tmp[:, sb_:sb_ + 1], EPS, None,
                                                ALU.add).then_inc(y_spread_ready, 1)
                    if on(k):
                        if on(f):
                            wait(dve, ln_chain, 2 * f + 1)
                            wait(dve, offset_ready, f - 3)
                        wait(dve, scores_done, k + 1)
                        nc.vector.tensor_reduce(out=top[:, u % 2, :], in_=ps_s[:, :].rearrange("p (h k) -> p h k", h=HEADS),
                                                op=ALU.max, axis=AX.X).then_inc(top_ready, 1)
                    if on(f):
                        if not on(k):
                            wait(dve, ln_chain, 2 * f + 1)
                            wait(dve, offset_ready, f - 3)
                        for n in range(NORMS):
                            last = nc.vector.bn_aggr(moments[:, sf, n, :], stats[:, sf, n, :])
                        last.then_inc(ln_chain, 1)
                    if on(j + 4):
                        wait(dve, rstd_ready, rstd_step(j - 1))
                        wait(dve, norm_ready, j + 1)
                        nc.vector.scalar_tensor_tensor(out=offset[:, u, 0:NORMS], in0=moments[:, u, 0:NORMS, 0], scalar=-1.0,
                                                       in1=rstd[:, u, 0:NORMS], op0=ALU.mult, op1=ALU.mult).then_inc(offset_ready, 1)
                    if on(f):
                        wait(dve, ln_chain, 2 * f + 2)
                        wait(dve, rstd_ready, rstd_step(j - 4))
                        if gated:
                            nc.vector.tensor_scalar(spread[:, sf, 0:1], moments[:, sf, 0, 1:2], 1.0 + EPS, EPS * EPS, ALU.mult, ALU.add)
                            nc.vector.tensor_scalar(spread[:, sf, 1:2], moments[:, sf, 1, 1:2], EPS, None, ALU.add).then_inc(spread_ready, 1)
                        else:
                            nc.vector.tensor_scalar(spread[:, sf, 0:1], moments[:, sf, 0, 1:2], EPS, None, ALU.add).then_inc(spread_ready, 1)
                    if on(k):
                        wait(dve, top_ready, k + 1)
                        wait(dve, prob_t_done, k - 1)
                        nc.vector.tensor_tensor(prob[:, u % 2, :].rearrange("p (h k) -> p h k", h=HEADS),
                                                ps_s[:, :].rearrange("p (h k) -> p h k", h=HEADS),
                                                top[:, u % 2, :].unsqueeze(2).to_broadcast([P, HEADS, SEQ]),
                                                ALU.subtract).then_inc(shifted, 1)

                steps.run(dve, step)


def split_products(nc, out, w_hi, w_lo, x_hi, x_lo, first, last):
    if w_lo is not None:
        nc.tensor.matmul(out, w_lo, x_hi, start=first, stop=False)
    nc.tensor.matmul(out, w_hi, x_lo, start=first and w_lo is None, stop=False)
    return nc.tensor.matmul(out, w_hi, x_hi, start=False, stop=last)


CHUNK_TILES = 4
CHUNK = CHUNK_TILES * P


def gated_feed_forward(nc, t):
    N = t.tiles // CHUNK_TILES
    steps = Steps(N, lead=2, lag=2, unroll=1)
    on = steps.on
    LEVELS = 3

    with ExitStack() as ctx:
        def sb(name, shape, dt=F32):
            return ctx.enter_context(nc.sbuf_tensor(f"g_{name}", shape, dt))

        def psum(name, n=1):
            return ctx.enter_context(nc.psum_tensor(f"g_{name}", [P, 512 * n], F32))

        def sem(name):
            return ctx.enter_context(nc.semaphore(f"g_{name}"))

        stats = sb("stats", [P, CHUNK_TILES, 6])
        moments = sb("moments", [P, CHUNK_TILES, 2])
        spread = sb("spread", [P, CHUNK_TILES])
        rstd = sb("rstd", [P, CHUNK_TILES])
        normed = sb("normed", [P, CHUNK_TILES, P])
        x_hi, x_lo = sb("x_hi", [P, CHUNK], F32R), sb("x_lo", [P, CHUNK], F32R)
        h = sb("h", [P, 2, CHUNK])
        silu = sb("silu", [P, 2, CHUNK])
        h_hi = [sb(f"h_hi{n}", [P, 4, CHUNK], F32R) for n in range(LEVELS)]
        h_lo = [sb(f"h_lo{n}", [P, 4, CHUNK], F32R) for n in range(LEVELS)]
        out_t = sb("out_t", [P, CHUNK])

        ps = psum("ps", 6)
        ps_in = psum("ps_in")
        ps_out = psum("ps_out")

        stats_chain = sem("stats_chain")
        spread_ready = sem("spread_ready")
        rstd_ready = sem("rstd_ready")
        norm_ready = sem("norm_ready")
        in_t_done = sem("in_t_done")
        x_hi_ready = sem("x_hi_ready")
        x_lo_ready = sem("x_lo_ready")
        done = [sem(f"done{n}") for n in range(LEVELS)]
        silu_ready = sem("silu_ready")
        act_ready = [sem(f"act_ready{n}") for n in range(LEVELS)]
        hi_ready = [sem(f"hi_ready{n}") for n in range(LEVELS)]
        lo_ready = [sem(f"lo_ready{n}") for n in range(LEVELS)]
        out_done = sem("out_done")
        out_taken = sem("out_taken")
        back_done = sem("back_done")
        x_done = sem("x_done")

        def bank(n):
            return ps[:, n * 512:(n + 1) * 512]

        def pair(o):
            return (4, 0, 2, 4)[o]

        with nc.Block() as block:
            @block.tensor
            def _(pe):
                def program(with_lo):
                    def w(g, cols):
                        return t.w_hi[:, g, cols], t.w_lo[:, g, cols] if with_lo else None

                    def turn_in(i):
                        if on(i):
                            wait(pe, norm_ready, i + 1)
                            wait(pe, x_lo_ready, i)
                            for k in range(CHUNK_TILES):
                                last = nc.tensor.transpose(ps_in[:, k * P:(k + 1) * P], normed[:, k, :], t.ident[:, :])
                            last.then_inc(in_t_done, 1)

                    def up(i, outputs):
                        if not on(i):
                            return
                        wait(pe, x_lo_ready, i + 1)
                        for o in outputs:
                            wait(pe, *((act_ready[0], 4 * i), (act_ready[1], 4 * i - 2),
                                       (act_ready[1], 4 * i), (act_ready[0], 4 * i + 1))[o])
                            for g in range(2):
                                last = split_products(nc, bank(pair(o) + g), *w(g, slice(o * P, (o + 1) * P)),
                                                      x_hi[:, :], x_lo[:, :], True, True)
                            last.then_inc(done[0], 1)

                    def middle(i, level):
                        if not on(i):
                            return
                        wait(pe, lo_ready[level - 1], 4 * i + 4)
                        for o in range(4):
                            if level == 1:
                                wait(pe, act_ready[2], 4 * (i - 1) + o + 1)
                            elif isinstance(i, int) and i + 1 >= N:
                                wait(pe, act_ready[1], 4 * i + o + 1)
                            else:
                                wait(pe, act_ready[0], 4 * (i + 1) + (2 if o < 2 else 3))
                            for c in range(4):
                                last = split_products(nc, bank(o), *w(2 + 4 * (level - 1) + c, slice(o * P, (o + 1) * P)),
                                                      h_hi[level - 1][:, c, :], h_lo[level - 1][:, c, :], c == 0, c == 3)
                            last.then_inc(done[level], 1)

                    def down(i):
                        if not on(i):
                            return
                        wait(pe, lo_ready[LEVELS - 1], 4 * i + 4)
                        wait(pe, x_done, i)
                        for c in range(4):
                            last = split_products(nc, ps_out[:, :], *w(10, slice(c * P, (c + 1) * P)),
                                                  h_hi[LEVELS - 1][:, c, :], h_lo[LEVELS - 1][:, c, :], c == 0, c == 3)
                        last.then_inc(out_done, 1)

                    def turn_back(i):
                        if on(i):
                            wait(pe, out_taken, i + 1)
                            for k in range(CHUNK_TILES):
                                last = nc.tensor.transpose(ps_out[:, k * P:(k + 1) * P], out_t[:, k * P:(k + 1) * P], t.ident[:, :])
                            last.then_inc(back_done, 1)

                    def step(j, u):
                        turn_in(j + 1)
                        middle(j, 1)
                        up(j + 1, (0, 1))
                        down(j - 1)
                        up(j + 1, (2, 3))
                        turn_back(j - 1)
                        middle(j, 2)

                    steps.run(pe, step)

                lo_bits = pe.value_load(t.lo_bits[0:1, 0:1].bitcast(I32))
                with pe.If(lo_bits):
                    program(with_lo=True)
                with pe.Else():
                    program(with_lo=False)

            @block.scalar
            def _(act):
                def hidden(i, level):
                    if not on(i):
                        return
                    for o in range(4):
                        wait(act, done[level], 4 * i + o + 1)
                        wait(act, lo_ready[level], 4 * i + o - 1)
                        if o < 2:
                            if level == 1:
                                wait(act, lo_ready[2], 4 * i)
                            elif isinstance(i, int) and i + 1 >= N:
                                wait(act, lo_ready[1], 4 * i + 4)
                            else:
                                wait(act, lo_ready[0], 4 * i + 8)
                        nc.scalar.activation(h[:, o % 2, :], bank(o), ACT.Gelu,
                                             scale=t.s[:, 1 + level, o:o + 1]).then_inc(act_ready[level], 1)
                        split_hi(i, level, o)

                def split_hi(i, level, o):
                    wait(act, act_ready[level], 4 * i + o + 1)
                    wait(act, *readers(i, level))
                    nc.scalar.activation(h_hi[level][:, o, :], h[:, o % 2, :], ACT.Copy).then_inc(hi_ready[level], 1)

                def readers(i, level):
                    if level == LEVELS - 1:
                        return out_done, i
                    return done[level + 1], 4 * i

                def take_in(i):
                    if on(i):
                        wait(act, in_t_done, i + 1)
                        wait(act, done[0], 4 * i)
                        nc.scalar.activation(x_hi[:, :], ps_in[:, :], ACT.Copy).then_inc(x_hi_ready, 1)

                def take_out(i):
                    if on(i):
                        wait(act, out_done, i + 1)
                        wait(act, back_done, i)
                        nc.scalar.activation(out_t[:, :], ps_out[:, :], ACT.Copy, scale=t.s3[:, 0:1]).then_inc(out_taken, 1)

                def silu_stage(i, after):
                    if not on(i):
                        take_out(after)
                        return
                    for o in range(4):
                        wait(act, done[0], 4 * i + o + 1)
                        wait(act, act_ready[0], 4 * i + o - 1)
                        nc.scalar.activation(silu[:, o % 2, :], bank(pair(o)), ACT.Silu,
                                             scale=t.s[:, 0, o:o + 1]).then_inc(silu_ready, 1)
                        if o > 0:
                            split_hi(i, 0, o - 1)
                        if o == 1:
                            take_out(after)
                    split_hi(i, 0, 3)

                def step(j, u):
                    take_in(j + 1)
                    hidden(j, 1)
                    silu_stage(j + 1, after=j - 1)
                    hidden(j, 2)

                steps.run(act, step)

            @block.gpsimd
            def _(pool):
                def step(j, u):
                    if on(j + 2):
                        wait(pool, spread_ready, j + 3)
                        wait(pool, norm_ready, j + 2)
                        nc.gpsimd.tensor_tensor(rstd[:, :], spread[:, :], t.minus_half[:, 0:CHUNK_TILES], ALU.pow).then_inc(rstd_ready, 1)

                steps.run(pool, step)

            @block.vector
            def _(dve):
                def split_lo(i, level, o):
                    wait(dve, hi_ready[level], 4 * i + o + 1)
                    nc.vector.tensor_tensor(h_lo[level][:, o, :], h[:, o % 2, :], h_hi[level][:, o, :].bitcast(F32),
                                            ALU.subtract).then_inc(lo_ready[level], 1)

                def measure(i):
                    for k in range(CHUNK_TILES):
                        last = nc.vector.bn_stats(stats[:, k, :], t.x[:, span(i * CHUNK_TILES + k, P)])
                    last.then_inc(stats_chain, 1)
                    wait(dve, stats_chain, 2 * i + 1)

                def moments_of(i):
                    for k in range(CHUNK_TILES):
                        last = nc.vector.bn_aggr(moments[:, k, :], stats[:, k, :])
                    last.then_inc(stats_chain, 1)
                    wait(dve, stats_chain, 2 * i + 2)
                    wait(dve, rstd_ready, i)
                    nc.vector.tensor_scalar(spread[:, :], moments[:, :, 1], EPS, None, ALU.add).then_inc(spread_ready, 1)

                def normalise(i):
                    if not on(i):
                        return
                    wait(dve, rstd_ready, i + 1)
                    wait(dve, in_t_done, i)
                    for k in range(CHUNK_TILES):
                        last = nc.vector.tensor_scalar(normed[:, k, :], t.x[:, span(i * CHUNK_TILES + k, P)], moments[:, k, 0:1],
                                                       rstd[:, k:k + 1], ALU.subtract, ALU.mult)
                    last.then_inc(norm_ready, 1)

                def split_in(i):
                    if on(i):
                        wait(dve, x_hi_ready, i + 1)
                        wait(dve, done[0], 4 * i)
                        nc.vector.tensor_tensor(x_lo[:, :], ps_in[:, :], x_hi[:, :].bitcast(F32), ALU.subtract).then_inc(x_lo_ready, 1)

                def product_stage(i):
                    if not on(i):
                        return
                    for o in range(4):
                        wait(dve, silu_ready, 4 * i + o + 1)
                        wait(dve, *((lo_ready[0], 4 * i + o - 1) if o > 1 else (lo_ready[1], 4 * i)))
                        nc.vector.scalar_tensor_tensor(out=h[:, o % 2, :], in0=bank(pair(o) + 1), scalar=t.s[:, 1, o:o + 1],
                                                       in1=silu[:, o % 2, :], op0=ALU.mult, op1=ALU.mult).then_inc(act_ready[0], 1)
                        if o > 0:
                            split_lo(i, 0, o - 1)
                    split_lo(i, 0, 3)

                def residual(i):
                    if on(i):
                        wait(dve, back_done, i + 1)
                        nc.vector.tensor_tensor(t.x[:, span(i, CHUNK)], ps_out[:, :], t.x[:, span(i, CHUNK)], ALU.add).then_inc(x_done, 1)

                def step(j, u):
                    split_in(j + 1)
                    if on(j + 2):
                        measure(j + 2)
                    if on(j):
                        split_lo(j, 1, 0)
                    if on(j + 2):
                        moments_of(j + 2)
                    if on(j):
                        for o in range(1, 4):
                            split_lo(j, 1, o)
                    product_stage(j + 1)
                    residual(j - 1)
                    normalise(j + 2)
                    if on(j):
                        for o in range(4):
                            split_lo(j, 2, o)

                steps.run(dve, step)


def plain_feed_forward(nc, t):
    N = t.tiles // CHUNK_TILES
    steps = Steps(N, lead=3, lag=3, unroll=2)
    on = steps.on

    with ExitStack() as ctx:
        def sb(name, shape, dt=F32):
            return ctx.enter_context(nc.sbuf_tensor(f"p_{name}", shape, dt))

        def psum(name, n=1):
            return ctx.enter_context(nc.psum_tensor(f"p_{name}", [P, 512 * n], F32))

        def sem(name):
            return ctx.enter_context(nc.semaphore(f"p_{name}"))

        stats = sb("stats", [P, 2, CHUNK_TILES, 6])
        moments = sb("moments", [P, 2, CHUNK_TILES, 2])
        spread = sb("spread", [P, 2, CHUNK_TILES])
        rstd = sb("rstd", [P, 2, CHUNK_TILES])
        normed = sb("normed", [P, 2, CHUNK_TILES, P])
        x_hi, x_lo = sb("x_hi", [P, 2, CHUNK], F32R), sb("x_lo", [P, 2, CHUNK], F32R)
        h = sb("h", [P, 4, CHUNK])
        h_hi, h_lo = sb("h_hi", [P, 2, 4, CHUNK], F32R), sb("h_lo", [P, 2, 4, CHUNK], F32R)
        out_t = sb("out_t", [P, 2, CHUNK])

        ps = psum("ps", 4)
        ps_in = psum("ps_in")
        ps_out = psum("ps_out", 2)
        ps_back = psum("ps_back")

        stats_chain = sem("stats_chain")
        spread_ready = sem("spread_ready")
        rstd_ready = sem("rstd_ready")
        norm_ready = sem("norm_ready")
        in_t_done = sem("in_t_done")
        x_hi_ready = sem("x_hi_ready")
        x_lo_ready = sem("x_lo_ready")
        up_done = sem("up_done")
        h_ready = sem("h_ready")
        hi_ready = sem("hi_ready")
        lo_ready = sem("lo_ready")
        out_done = sem("out_done")
        out_taken = sem("out_taken")
        back_done = sem("back_done")
        x_done = sem("x_done")
        stored = sem("stored")

        def bank(of, n):
            return of[:, n * 512:(n + 1) * 512]

        with nc.Block() as block:
            @block.tensor
            def _(pe):
                def step(j, u):
                    if on(j):
                        wait(pe, x_lo_ready, j + 1)
                        for o in range(4):
                            cols = slice(o * P, (o + 1) * P)
                            wait(pe, h_ready, 4 * (j - 1) + o + 1)
                            last = split_products(nc, bank(ps, o), t.f1_hi[:, 0, cols], t.f1_lo[:, 0, cols],
                                                  x_hi[:, u, :], x_lo[:, u, :], True, True)
                            last.then_inc(up_done, 1)
                    i, s = j + 1, 1 - u
                    if on(i):
                        wait(pe, norm_ready, i + 1)
                        wait(pe, x_lo_ready, i)
                        for k in range(CHUNK_TILES):
                            last = nc.tensor.transpose(ps_in[:, k * P:(k + 1) * P], normed[:, s, k, :], t.ident[:, :])
                        last.then_inc(in_t_done, 1)
                    i, s = j - 1, 1 - u
                    if on(i):
                        wait(pe, lo_ready, 4 * i + 4)
                        wait(pe, out_taken, i - 1)
                        for c in range(4):
                            cols = slice(c * P, (c + 1) * P)
                            last = split_products(nc, bank(ps_out, s), t.f1_hi[:, 1, cols], t.f1_lo[:, 1, cols],
                                                  h_hi[:, s, c, :], h_lo[:, s, c, :], c == 0, c == 3)
                        last.then_inc(out_done, 1)
                    i, s = j - 2, u
                    if on(i):
                        wait(pe, out_taken, i + 1)
                        wait(pe, x_done, i)
                        for k in range(CHUNK_TILES):
                            last = nc.tensor.transpose(ps_back[:, k * P:(k + 1) * P], out_t[:, s, k * P:(k + 1) * P], t.ident[:, :])
                        last.then_inc(back_done, 1)

                steps.run(pe, step)

            @block.scalar
            def _(act):
                def step(j, u):
                    i, s = j - 2, u
                    if on(i):
                        wait(act, out_done, i + 1)
                        wait(act, back_done, i - 1)
                        nc.scalar.activation(out_t[:, s, :], bank(ps_out, s), ACT.Identity, bias=t.b2[:, 0:1]).then_inc(out_taken, 1)
                    if on(j):
                        wait(act, out_done, j - 1)
                    for o in range(5):
                        if on(j) and o < 4:
                            wait(act, up_done, 4 * j + o + 1)
                            wait(act, lo_ready, 4 * j + o - 3)
                            nc.scalar.activation(h[:, o, :], bank(ps, o), ACT.Relu, bias=t.b1[:, o:o + 1]).then_inc(h_ready, 1)
                        if on(j) and o > 0:
                            wait(act, h_ready, 4 * j + o)
                            nc.scalar.activation(h_hi[:, u, o - 1, :], h[:, o - 1, :], ACT.Copy).then_inc(hi_ready, 1)
                        i, s = j + 1, 1 - u
                        if on(i) and o == 2:
                            wait(act, in_t_done, i + 1)
                            wait(act, up_done, 4 * (i - 1))
                            nc.scalar.activation(x_hi[:, s, :], ps_in[:, :], ACT.Copy).then_inc(x_hi_ready, 1)

                steps.run(act, step)

            @block.gpsimd
            def _(pool):
                def step(j, u):
                    i, s = j + 3, 1 - u
                    if on(i):
                        wait(pool, spread_ready, i + 1)
                        wait(pool, norm_ready, i - 1)
                        nc.gpsimd.tensor_tensor(rstd[:, s, :], spread[:, s, :], t.minus_half[:, 0:CHUNK_TILES], ALU.pow).then_inc(rstd_ready, 1)

                steps.run(pool, step)

            @block.vector
            def _(dve):
                def split_lo(i, s, o):
                    wait(dve, hi_ready, 4 * i + o + 1)
                    nc.vector.tensor_tensor(h_lo[:, s, o, :], h[:, o, :], h_hi[:, s, o, :].bitcast(F32),
                                            ALU.subtract).then_inc(lo_ready, 1)

                def step(j, u):
                    i, s = j - 3, 1 - u
                    if on(i):
                        wait(dve, back_done, i + 1)
                        nc.vector.tensor_tensor(t.x[:, span(i, CHUNK)], ps_back[:, :], t.x[:, span(i, CHUNK)], ALU.add).then_inc(x_done, 1)
                    i, s = j + 3, 1 - u
                    if on(i):
                        for k in range(CHUNK_TILES):
                            last = nc.vector.bn_stats(stats[:, s, k, :], t.x[:, span(i * CHUNK_TILES + k, P)])
                        last.then_inc(stats_chain, 1)
                        wait(dve, stats_chain, 2 * i + 1)
                        wait(dve, norm_ready, i - 1)
                    if on(j):
                        wait(dve, out_done, j - 1)
                        split_lo(j, u, 0)
                    if on(i):
                        for k in range(CHUNK_TILES):
                            last = nc.vector.bn_aggr(moments[:, s, k, :], stats[:, s, k, :])
                        last.then_inc(stats_chain, 1)
                    if on(j):
                        split_lo(j, u, 1)
                    if on(i):
                        wait(dve, stats_chain, 2 * i + 2)
                        wait(dve, rstd_ready, i - 1)
                        nc.vector.tensor_scalar(spread[:, s, :], moments[:, s, :, 1], EPS, None, ALU.add).then_inc(spread_ready, 1)
                    i, s = j + 1, 1 - u
                    if on(i):
                        wait(dve, x_hi_ready, i + 1)
                        nc.vector.tensor_tensor(x_lo[:, s, :], ps_in[:, :], x_hi[:, s, :].bitcast(F32), ALU.subtract).then_inc(x_lo_ready, 1)
                    i, s = j + 2, u
                    if on(i):
                        wait(dve, rstd_ready, i + 1)
                        wait(dve, in_t_done, i - 1)
                        for k in range(CHUNK_TILES):
                            last = nc.vector.tensor_scalar(normed[:, s, k, :], t.x[:, span(i * CHUNK_TILES + k, P)], moments[:, s, k, 0:1],
                                                           rstd[:, s, k:k + 1], ALU.subtract, ALU.mult)
                        last.then_inc(norm_ready, 1)
                    if on(j):
                        split_lo(j, u, 2)
                        split_lo(j, u, 3)

                steps.run(dve, step)

            @block.sync
            def _(sp):
                xs = t.x[:, :].rearrange("p (t d) -> p t d", d=P)
                with sp.Fori(0, N) as i:
                    wait(sp, x_done, i + 1)
                    sp.dma_start(t.out.rearrange("(t b) s d -> (b s) t d", b=PER_TILE)[:, bass.ds(i * CHUNK_TILES, CHUNK_TILES), :],
                                 xs[:, bass.ds(i * CHUNK_TILES, CHUNK_TILES), :]).then_inc(stored, 16)
                sp.wait_ge(stored, 16 * N)


class Tensors:
    pass


def two_layer_xattn_ffn(nc, a, out):
    with ExitStack() as ctx:
        def sb(name, shape, dt=F32):
            return ctx.enter_context(nc.sbuf_tensor(name, shape, dt))

        t = Tensors()
        t.out = out
        t.tiles = a["x"].shape[0] // PER_TILE
        t.x = sb("x_res", [P, t.tiles * P])
        t.ctx = sb("ctx_res", [P, t.tiles * P])
        t.ident = sb("ident", [P, P])
        t.head_mask = sb("head_mask", [P, HEADS])
        t.minus_half = sb("minus_half", [P, 4])
        t.v_by_pair = sb("v_by_pair", [P, UNROLL, PER_TILE * PAIRS, PAIR_COLS])
        t.wa = sb("wa", [P, 2, 4, P])
        t.qk_bias = sb("qk_bias", [P, 2, 2])
        t.bias_row = sb("bias_row", [P, 2, P])
        t.ln_o_g = sb("ln_o_g", [P, P])
        t.ln_o_b = sb("ln_o_b", [P, P])
        t.gate_w = sb("gate_w", [P, 1])
        t.gate_nb = sb("gate_nb", [P, 1])
        t.w_hi = sb("w_hi", [P, 11, 512], F32R)
        t.w_lo = sb("w_lo", [P, 11, 512], F32R)
        t.lo_bits = sb("lo_bits", [P, 1])
        t.f1_hi = sb("f1_hi", [P, 2, 512], F32R)
        t.f1_lo = sb("f1_lo", [P, 2, 512], F32R)
        t.s = sb("s", [P, 4, 4])
        t.s3 = sb("s3", [P, 1])
        t.b1 = sb("b1", [P, 4])
        t.b2 = sb("b2", [P, 1])

        prepare(nc, t, a)
        attention(nc, t, 0)
        gated_feed_forward(nc, t)
        attention(nc, t, 1)
        plain_feed_forward(nc, t)


def kernel(**inputs):
    import numpy as np
    import concourse.bacc as bacc
    from concourse.bass_utils import run_bass_kernel_spmd

    nc = bacc.Bacc("TRN2", target_bir_lowering=False, num_devices=1)
    arrays, args = {}, {}
    for name, value in inputs.items():
        array = np.ascontiguousarray(value)
        arrays[f"in_{name}"] = array
        args[name] = nc.dram_tensor(f"in_{name}", array.shape, mybir.dt.from_np(array.dtype), kind="ExternalInput").ap()
    x = inputs["x"]
    out = nc.dram_tensor("out_x", x.shape, F32, kind="ExternalOutput").ap()
    two_layer_xattn_ffn(nc, args, out)
    r = run_bass_kernel_spmd(nc, [arrays], core_ids=[0])
    return r.results[0]["out_x"]
```

```python
from contextlib import ExitStack

import concourse.bass as bass
from concourse import mybir

ALU = mybir.AluOpType
ACT = mybir.ActivationFunctionType
AX = mybir.AxisListType
F32 = mybir.dt.float32
F32R = mybir.dt.float32r
I32 = mybir.dt.int32

P = 128
EPS = 1e-5
HEADS = 16
HEAD_DIM = 8
SEQ = 64
PER_TILE = P // SEQ
PAIRS = HEADS // 2
PAIR_COLS = 32
UNROLL = 4


def wait(eng, sem, count):
    if isinstance(count, int) and count <= 0:
        return
    eng.wait_ge(sem, count)


def span(i, width):
    return slice(i * width, (i + 1) * width) if isinstance(i, int) else bass.ds(i * width, width)


class Steps:

    def __init__(self, total, lead, lag, unroll):
        self.total, self.first, self.last, self.unroll = total, -lead, total + lag, unroll
        self.lo = -(-lag // unroll) * unroll
        self.hi = (total - lead) // unroll * unroll

    def run(self, eng, step):
        for j in range(self.first, self.lo):
            step(j, j % self.unroll)
        with eng.Fori(self.lo, self.hi, self.unroll) as base:
            for u in range(self.unroll):
                step(base + u, u)
        for j in range(self.hi, self.last):
            step(j, j % self.unroll)

    def on(self, i):
        return not isinstance(i, int) or 0 <= i < self.total


CHUNK_TILES = 4
CHUNK = CHUNK_TILES * P


class Front:

    def __init__(self, nc, ctx, name, slots):
        def sb(part, shape, dt=F32):
            return ctx.enter_context(nc.sbuf_tensor(f"{name}_{part}", shape, dt))

        def sem(part):
            return ctx.enter_context(nc.semaphore(f"{name}_{part}"))

        self.slots = slots
        self.stats = sb("stats", [P, slots, CHUNK_TILES, 6])
        self.moments = sb("moments", [P, slots, CHUNK_TILES, 2])
        self.spread = sb("spread", [P, slots, CHUNK_TILES])
        self.rstd = sb("rstd", [P, slots, CHUNK_TILES])
        self.normed = sb("normed", [P, slots, CHUNK_TILES, P])
        self.x_hi, self.x_lo = sb("x_hi", [P, slots, CHUNK], F32R), sb("x_lo", [P, slots, CHUNK], F32R)
        self.stats_chain = sem("stats_chain")
        self.spread_ready = sem("spread_ready")
        self.rstd_ready = sem("rstd_ready")
        self.norm_ready = sem("norm_ready")
        self.in_t_done = sem("in_t_done")
        self.x_hi_ready = sem("x_hi_ready")
        self.x_lo_ready = sem("x_lo_ready")
        self.up_done = sem("up_done")


def front_measure(nc, t, front, dve, i, s):
    for k in range(CHUNK_TILES):
        last = nc.vector.bn_stats(front.stats[:, s, k, :], t.x[:, span(i * CHUNK_TILES + k, P)])
    last.then_inc(front.stats_chain, 1)
    wait(dve, front.stats_chain, 2 * i + 1)
    wait(dve, front.norm_ready, i + 1 - front.slots)


def front_moments(nc, t, front, dve, i, s):
    for k in range(CHUNK_TILES):
        last = nc.vector.bn_aggr(front.moments[:, s, k, :], front.stats[:, s, k, :])
    last.then_inc(front.stats_chain, 1)


def front_spread(nc, t, front, dve, i, s):
    wait(dve, front.stats_chain, 2 * i + 2)
    wait(dve, front.rstd_ready, i + 1 - front.slots)
    nc.vector.tensor_scalar(front.spread[:, s, :], front.moments[:, s, :, 1], EPS, None, ALU.add).then_inc(front.spread_ready, 1)


def front_power(nc, t, front, pool, i, s):
    wait(pool, front.spread_ready, i + 1)
    wait(pool, front.norm_ready, i + 1 - front.slots)
    nc.gpsimd.tensor_tensor(front.rstd[:, s, :], front.spread[:, s, :], t.minus_half[:, 0:CHUNK_TILES],
                            ALU.pow).then_inc(front.rstd_ready, 1)


def front_normalise(nc, t, front, dve, i, s):
    wait(dve, front.rstd_ready, i + 1)
    wait(dve, front.in_t_done, i + 1 - front.slots)
    for k in range(CHUNK_TILES):
        last = nc.vector.tensor_scalar(front.normed[:, s, k, :], t.x[:, span(i * CHUNK_TILES + k, P)],
                                       front.moments[:, s, k, 0:1], front.rstd[:, s, k:k + 1], ALU.subtract, ALU.mult)
    last.then_inc(front.norm_ready, 1)


def front_turn_in(nc, t, front, pe, i, s, bank):
    wait(pe, front.norm_ready, i + 1)
    wait(pe, front.x_lo_ready, i)
    for k in range(CHUNK_TILES):
        last = nc.tensor.transpose(bank[:, k * P:(k + 1) * P], front.normed[:, s, k, :], t.ident[:, :])
    last.then_inc(front.in_t_done, 1)


def front_take_in(nc, t, front, act, i, s, bank):
    wait(act, front.in_t_done, i + 1)
    wait(act, front.up_done, 4 * (i + 1 - front.slots))
    nc.scalar.activation(front.x_hi[:, s, :], bank, ACT.Copy).then_inc(front.x_hi_ready, 1)


def front_split_in(nc, t, front, dve, i, s, bank):
    wait(dve, front.x_hi_ready, i + 1)
    nc.vector.tensor_tensor(front.x_lo[:, s, :], bank, front.x_hi[:, s, :].bitcast(F32), ALU.subtract).then_inc(front.x_lo_ready, 1)


def column(a):
    return a.rearrange("(p a) -> p a", a=1)


def row_everywhere(a):
    return a.rearrange("(a n) -> a n", a=1).to_broadcast([P, P])


def prepare(nc, t, a):
    with ExitStack() as ctx:
        def sb(name, shape, dt=F32):
            return ctx.enter_context(nc.sbuf_tensor(name, shape, dt))

        def sem(name):
            return ctx.enter_context(nc.semaphore(name))

        raw_up = sb("raw_up", [P, 2, 4, P])
        raw_mid = sb("raw_mid", [P, 2, 4, 512])
        raw_down = sb("raw_down", [P, 512])
        raw_l1 = sb("raw_l1", [P, 4, P])
        raw_l0 = sb("raw_l0", [P, 4, P])
        raw_w1 = sb("raw_w1", [P, 512])
        raw_w2 = sb("raw_w2", [P, 4, P])
        cols = sb("cols", [P, 10])
        rows = sb("rows", [P, 3, P])
        sums = sb("sums", [P, 2])
        vb = sb("vb", [P, 2])
        vb_wide = sb("vb_wide", [P, 2, P])
        ps = ctx.enter_context(nc.psum_tensor("prep_ps", [P, 4, 512], F32))
        ps_b = ctx.enter_context(nc.psum_tensor("prep_ps_b", [P, 512], F32))
        ps_r = ctx.enter_context(nc.psum_tensor("prep_ps_r", [P, 2, 512], F32))

        params_loaded, rows_loaded = sem("params_loaded"), sem("rows_loaded")
        l0_weights_loaded, l1_weights_loaded = sem("l0_weights_loaded"), sem("l1_weights_loaded")
        ff0_weights_loaded = [sem(f"ff0_weights_loaded{g}") for g in range(5)]
        ff1_weights_loaded = sem("ff1_weights_loaded")
        zeros_ready, ident_ready, consts_ready = sem("zeros_ready"), sem("ident_ready"), sem("consts_ready")
        v_zero_ready = sem("v_zero_ready")
        turned = sem("turned")
        hi_taken, lo_taken = sem("hi_taken"), sem("lo_taken")
        l1_turned_taken = sem("l1_turned_taken")
        bias_done, bias_row_done = sem("bias_done"), sem("bias_row_done")
        value_bias_ready = sem("value_bias_ready")
        chain = sem("prep_chain")

        with nc.Block() as block:
            @block.sync
            def _(sp):
                xv = a["x"].rearrange("(t b) s d -> (b s) t d", b=PER_TILE)
                cv = a["ctx_1024"].rearrange("(t b) s d -> (b s) t d", b=PER_TILE)
                xs = t.x[:, :].rearrange("p (t d) -> p t d", d=P)
                cs = t.ctx[:, :].rearrange("p (t d) -> p t d", d=P)

                def load_tiles(n):
                    first, last = (t.load_steps + [t.tiles])[n:n + 2]
                    sp.dma_start(xs[:, first:last, :], xv[:, first:last, :]).then_inc(t.tiles_loaded[n], 16)
                    sp.dma_start(cs[:, first:last, :], cv[:, first:last, :]).then_inc(t.tiles_loaded[n], 16)

                for n, k in enumerate(("Wq", "Wk", "Wv", "Wo")):
                    sp.dma_start(raw_l0[:, n, :], a[f"L0_xattn_{k}"]).then_inc(l0_weights_loaded, 16)
                for n, k in enumerate(("w1", "w2", "h1", "h2")):
                    rows_in = a[f"L0_ffn_{k}_w"].rearrange("(r p) i -> p r i", p=P)
                    dst = raw_up[:, n, :, :] if n < 2 else raw_mid[:, n - 2, :, :]
                    sp.dma_start(dst, rows_in).then_inc(ff0_weights_loaded[n], 16)
                sp.dma_start(raw_down[:, :], a["L0_ffn_w3_w"]).then_inc(ff0_weights_loaded[4], 16)
                for n, k in enumerate(("w_q", "w_k", "w_v", "w_o")):
                    sp.dma_start(raw_l1[:, n, :], a[f"L1_xattn_{k}"]).then_inc(l1_weights_loaded, 16)
                load_tiles(0)
                sp.dma_start(raw_w1[:, :], a["L1_ffn_W1"]).then_inc(ff1_weights_loaded, 16)
                sp.dma_start(raw_w2[:, :, :], a["L1_ffn_W2"].rearrange("(c p) o -> p c o", p=P)).then_inc(ff1_weights_loaded, 16)
                for n in range(1, len(t.load_steps)):
                    load_tiles(n)

            @block.scalar
            def _(act):
                names = ["L0_xattn_bq", "L0_xattn_bk", "L0_xattn_bv", "L0_xattn_ln_q_g", "L0_xattn_ln_q_b",
                         "L0_xattn_ln_kv_g", "L0_xattn_ln_kv_b", "L1_xattn_b_q", "L1_xattn_b_k", "L1_xattn_b_v"]
                for n, k in enumerate(names):
                    act.dma_start(cols[:, n:n + 1], column(a[k])).then_inc(params_loaded, 16)
                act.dma_start(rows[:, 0, :], row_everywhere(a["L0_xattn_Wg"].rearrange("d a -> (d a)"))).then_inc(params_loaded, 16)
                act.dma_start(rows[:, 1, :], row_everywhere(a["L0_xattn_ln_q_b"])).then_inc(params_loaded, 16)
                act.dma_start(rows[:, 2, :], row_everywhere(a["L0_xattn_ln_q_g"])).then_inc(params_loaded, 16)
                for g in range(11):
                    act.wait_ge(turned, g + 1)
                    act.activation(t.w_hi[:, g, :], ps[:, g % 4, :], ACT.Copy).then_inc(hi_taken, 1)
                act.wait_ge(turned, 12)
                for n in (0, 1, 3):
                    act.activation(t.wa[:, 1, n, :], ps[:, 3, n * P:(n + 1) * P], ACT.Copy)
                act.activation(t.wa[:, 1, 2, :].rearrange("p (q c d) -> p q c d", q=2, d=HEAD_DIM),
                               ps[:, 3, 2 * P:3 * P].rearrange("p (c q d) -> p q c d", q=2, d=HEAD_DIM), ACT.Copy).then_inc(l1_turned_taken, 1)
                act.wait_ge(ff1_weights_loaded, 32)
                act.activation(t.f1_hi[:, 0, :], raw_w1[:, :], ACT.Copy)
                act.activation(t.f1_hi[:, 1, :], raw_w2[:, :, :], ACT.Copy).then_inc(hi_taken, 1)

            @block.gpsimd
            def _(pool):
                nc.gpsimd.memset(t.ident[:, :], 0.0).then_inc(zeros_ready, 1)
                nc.gpsimd.memset(t.head_mask[:, :], 1.0).then_inc(zeros_ready, 1)
                nc.gpsimd.memset(t.minus_half[:, :], -0.5)
                pool.wait_ge(zeros_ready, 2)
                nc.gpsimd.affine_select(out=t.ident[:, :], in_=t.ident[:, :], compare_op=ALU.not_equal, fill=1.0,
                                        base=0, pattern=[[-1, P]], channel_multiplier=1).then_inc(ident_ready, 1)
                nc.gpsimd.affine_select(out=t.head_mask[:, :], in_=t.head_mask[:, :], compare_op=ALU.is_ge, fill=0.0,
                                        base=0, pattern=[[-HEAD_DIM, HEADS]], channel_multiplier=1).then_inc(consts_ready, 1)
                pool.wait_ge(consts_ready, 1)
                nc.gpsimd.affine_select(out=t.head_mask[:, :], in_=t.head_mask[:, :], compare_op=ALU.is_ge, fill=0.0,
                                        base=HEAD_DIM - 1, pattern=[[HEAD_DIM, HEADS]], channel_multiplier=-1).then_inc(consts_ready, 1)
                pool.dma_start(t.bias_row[:, 0, :], row_everywhere(a["L0_xattn_bo"])).then_inc(rows_loaded, 16)
                pool.dma_start(t.bias_row[:, 1, :], row_everywhere(a["L1_xattn_b_o"])).then_inc(rows_loaded, 16)
                pool.dma_start(t.ln_o_g[:, :], row_everywhere(a["L0_xattn_ln_o_g"])).then_inc(rows_loaded, 16)
                pool.dma_start(t.ln_o_b[:, :], row_everywhere(a["L0_xattn_ln_o_b"])).then_inc(rows_loaded, 16)
                for n, k in enumerate(("w1_s", "w2_s", "h1_s", "h2_s")):
                    pool.dma_start(t.s[:, n, :], a[f"L0_ffn_{k}"].rearrange("(o p) -> p o", p=P),
                                   allow_slow_non_contiguous=True).then_inc(t.scales_loaded, 16)
                pool.dma_start(t.s3[:, :], column(a["L0_ffn_w3_s"])).then_inc(t.scales_loaded, 16)
                pool.dma_start(t.b1[:, :], a["L1_ffn_b1"].rearrange("(o p) -> p o", p=P),
                               allow_slow_non_contiguous=True).then_inc(t.scales_loaded, 16)
                pool.dma_start(t.b2[:, :], column(a["L1_ffn_b2"])).then_inc(t.scales_loaded, 16)
                pool.wait_ge(rows_loaded, 64)

            @block.tensor
            def _(pe):
                pe.wait_ge(ident_ready, 1)
                for g in range(11):
                    matrix = g if g < 2 else 2 + (g - 2) // 4
                    blocks = [raw_up[:, g, r, :] if g < 2 else raw_down[:, r * P:(r + 1) * P] if g == 10
                              else raw_mid[:, matrix - 2, r, (g - 2) % 4 * P:((g - 2) % 4 + 1) * P] for r in range(4)]
                    pe.wait_ge(ff0_weights_loaded[matrix], 16)
                    if g >= 4:
                        pe.wait_ge(hi_taken, g - 3)
                        pe.wait_ge(lo_taken, g - 3)
                    for r in range(4):
                        last = nc.tensor.transpose(ps[:, g % 4, r * P:(r + 1) * P], blocks[r], t.ident[:, :])
                    last.then_inc(turned, 1)
                pe.wait_ge(l1_weights_loaded, 64)
                pe.wait_ge(hi_taken, 8)
                pe.wait_ge(lo_taken, 8)
                for r in range(4):
                    last = nc.tensor.transpose(ps[:, 3, r * P:(r + 1) * P], raw_l1[:, r, :], t.ident[:, :])
                last.then_inc(turned, 1)
                pe.wait_ge(l0_weights_loaded, 64)
                pe.wait_ge(params_loaded, 16 * 13)
                nc.tensor.matmul(ps_b[:, 0:1], raw_l0[:, 0, :], cols[:, 4:5], start=True, stop=True)
                nc.tensor.matmul(ps_b[:, 1:2], raw_l0[:, 1, :], cols[:, 6:7], start=True, stop=True)
                nc.tensor.matmul(ps_b[:, 2:3], raw_l0[:, 2, :], cols[:, 6:7], start=True, stop=True).then_inc(bias_done, 1)
                pe.wait_ge(value_bias_ready, 1)
                nc.tensor.matmul(ps_r[:, 0, 0:P], vb_wide[:, 0, :], raw_l0[:, 3, :], start=True, stop=True)
                pe.wait_ge(l1_turned_taken, 1)
                nc.tensor.matmul(ps_r[:, 1, 0:P], vb_wide[:, 1, :], t.wa[:, 1, 3, :], start=True, stop=True).then_inc(bias_row_done, 1)

            @block.vector
            def _(dve):
                s = float(HEAD_DIM) ** -0.5
                nc.vector.memset(t.v_by_pair[:, :, :, :], 0.0).then_inc(v_zero_ready, 1)
                dve.wait_ge(v_zero_ready, 1)
                for h2 in range(2):
                    c0 = 2 * HEAD_DIM + h2
                    nc.vector.memset(t.v_by_pair[h2 * SEQ:(h2 + 1) * SEQ, :, :, c0:c0 + 1], 1.0)
                for g in range(11):
                    dve.wait_ge(hi_taken, g + 1)
                    nc.vector.tensor_tensor(t.w_lo[:, g, :], ps[:, g % 4, :], t.w_hi[:, g, :].bitcast(F32), ALU.subtract).then_inc(lo_taken, 1)
                dve.wait_ge(l0_weights_loaded, 64)
                dve.wait_ge(params_loaded, 16 * 13)
                nc.vector.tensor_scalar(t.wa[:, 0, 0, :], raw_l0[:, 0, :], cols[:, 3:4], s, ALU.mult, ALU.mult)
                nc.vector.tensor_scalar(t.wa[:, 0, 1, :], raw_l0[:, 1, :], cols[:, 5:6], None, ALU.mult)
                by_half = "p (q c d) -> p q c d", "p (c q d) -> p q c d"
                nc.vector.tensor_scalar(t.wa[:, 0, 2, :].rearrange(by_half[0], q=2, d=HEAD_DIM),
                                        raw_l0[:, 2, :].rearrange(by_half[1], q=2, d=HEAD_DIM), cols[:, 5:6], None, ALU.mult)
                nc.vector.tensor_copy(t.wa[:, 0, 3, :], raw_l0[:, 3, :])
                nc.vector.tensor_tensor(t.gate_w[:, :], rows[:, 0, :], rows[:, 2, :], ALU.mult)
                nc.vector.tensor_tensor_reduce(out=vb_wide[:, 0, :], in0=rows[:, 0, :], in1=rows[:, 1, :], scale=1.0, scalar=0.0,
                                               op0=ALU.mult, op1=ALU.add, accum_out=sums[:, 0:1]).then_inc(chain, 1)
                dve.wait_ge(chain, 1)
                nc.vector.tensor_scalar(t.gate_nb[:, :], sums[:, 0:1], -1.0, None, ALU.mult)
                dve.wait_ge(bias_done, 1)
                nc.vector.tensor_tensor(sums[:, 1:2], ps_b[:, 0:1], cols[:, 0:1], ALU.add)
                nc.vector.tensor_tensor(t.qk_bias[:, 0, 1:2], ps_b[:, 1:2], cols[:, 1:2], ALU.add)
                nc.vector.tensor_tensor(vb[:, 0:1], ps_b[:, 2:3], cols[:, 2:3], ALU.add)
                nc.vector.tensor_copy(vb[:, 1:2], cols[:, 9:10])
                nc.vector.tensor_scalar(t.qk_bias[:, 1, 0:1], cols[:, 7:8], s, None, ALU.mult)
                nc.vector.tensor_copy(t.qk_bias[:, 1, 1:2], cols[:, 8:9]).then_inc(chain, 1)
                dve.wait_ge(chain, 2)
                nc.vector.tensor_scalar(t.qk_bias[:, 0, 0:1], sums[:, 1:2], s, None, ALU.mult)
                nc.vector.tensor_copy(vb_wide[:, :, :], vb[:, :].unsqueeze(2).to_broadcast([P, 2, P])).then_inc(value_bias_ready, 1)
                dve.wait_ge(hi_taken, 12)
                nc.vector.tensor_tensor(t.f1_lo[:, 0, :], raw_w1[:, :],
                                        t.f1_hi[:, 0, :].bitcast(F32), ALU.subtract)
                nc.vector.tensor_tensor(t.f1_lo[:, 1, :], raw_w2[:, :, :].rearrange("p o i -> p (o i)"),
                                        t.f1_hi[:, 1, :].bitcast(F32), ALU.subtract)
                dve.wait_ge(rows_loaded, 64)
                dve.wait_ge(bias_row_done, 1)
                nc.vector.tensor_tensor(t.bias_row[:, 0, :], t.bias_row[:, 0, :], ps_r[:, 0, 0:P], ALU.add)
                nc.vector.tensor_tensor(t.bias_row[:, 1, :], t.bias_row[:, 1, :], ps_r[:, 1, 0:P], ALU.add)
                nc.vector.tensor_scalar(t.wa[:, 1, 0, :], t.wa[:, 1, 0, :], s, None, ALU.mult)


def attention(nc, t, layer, front):
    gated = layer == 0
    T = t.tiles
    steps = Steps(T, lead=5, lag=9, unroll=UNROLL)
    on = steps.on
    wq, wk, wv, wo = (t.wa[:, layer, n, :] for n in range(4))

    with ExitStack() as ctx:
        def sb(name, shape, dt=F32):
            return ctx.enter_context(nc.sbuf_tensor(f"{name}{layer}", shape, dt))

        def psum(name, n=1):
            return ctx.enter_context(nc.psum_tensor(f"{name}{layer}", [P, 512 * n], F32))

        def sem(name):
            return ctx.enter_context(nc.semaphore(f"{name}{layer}"))

        stats = sb("stats", [P, UNROLL, 2, 6])
        moments = sb("moments", [P, UNROLL, 2, 2])
        spread = sb("spread", [P, UNROLL, 3])
        rstd = sb("rstd", [P, UNROLL, 3])
        offset = sb("offset", [P, UNROLL, 2])
        normed = sb("normed", [P, UNROLL, 2, P])
        turned = sb("turned", [P, 2, 2, P])
        q_t = sb("q_t", [P, UNROLL, P])
        k_t = sb("k_t", [P, UNROLL, P])
        k_heads = sb("k_heads", [P, 2, HEADS, P])
        top = sb("top", [P, 2, HEADS])
        prob = sb("prob", [P, 2, HEADS * SEQ])
        prob_t = sb("prob_t", [P, 2, PAIRS, P])
        sums_t = sb("sums_t", [P, 2, 2, P])
        rden = sb("rden", [P, 2, PAIRS, 2])
        heads_out = sb("heads_out", [P, 2, P])
        out_t = sb("out_t", [P, 2, P])
        if gated:
            gate_prod = sb("gate_prod", [P, P])
            gate_in = sb("gate_in", [P, UNROLL])
            gate_exp = sb("gate_exp", [P, T])
            gate = sb("gate", [P, UNROLL])
            y = sb("y", [P, UNROLL, P])
            y_stats = sb("y_stats", [P, 6])
            y_moments = sb("y_moments", [P, UNROLL, 2])
            y_tmp = sb("y_tmp", [P, UNROLL])
            y_scale = sb("y_scale", [P, 1])
            y_gain = sb("y_gain", [P, P])
            lo_abs = sb("lo_abs", [P, 11 * P])

        ps_s = psum("ps_s", 2)
        ps_pt = psum("ps_pt", 2)
        ps_in = psum("ps_in")
        ps_qkv = psum("ps_qkv")
        ps_o = psum("ps_o")
        ps_y = psum("ps_y")

        ln_chain = sem("ln_chain")
        spread_ready = sem("spread_ready")
        rstd_ready = sem("rstd_ready")
        offset_ready = sem("offset_ready")
        norm_ready = sem("norm_ready")
        in_t_done = sem("in_t_done")
        in_t_taken = sem("in_t_taken")
        qkv_done = sem("qkv_done")
        k_taken = sem("k_taken")
        qkv_taken = sem("qkv_taken")
        k_heads_ready = sem("k_heads_ready")
        scores_done = sem("scores_done")
        top_ready = sem("top_ready")
        shifted = sem("shifted")
        exp_done = sem("exp_done")
        prob_t_done = sem("prob_t_done")
        prob_t_taken = sem("prob_t_taken")
        pv_done = sem("pv_done")
        sums_taken = sem("sums_taken")
        sums_back = sem("sums_back")
        rden_ready = sem("rden_ready")
        heads_ready = sem("heads_ready")
        heads_t_done = sem("heads_t_done")
        out_t_ready = sem("out_t_ready")
        y_done = sem("y_done")
        y_taken = sem("y_taken")
        biased = sem("biased")
        z_ready = sem("z_ready")
        gate_exp_ready = sem("gate_exp_ready")
        y_chain = sem("y_chain")
        y_spread_ready = sem("y_spread_ready")
        lo_summed = sem("lo_summed")
        y2_chain = sem("y2_chain")
        x_done = sem("x_done")

        closing_row = t.ln_o_b[:, :] if gated else t.bias_row[:, 1, :]
        NORMS = 2 if gated else 1

        def upto(count):
            return min(count, T) if isinstance(count, int) else count

        def rstd_step(j):
            return j + 6

        with nc.Block() as block:
            @block.tensor
            def _(pe):
                def step(j, u):
                    if on(j):
                        wait(pe, qkv_taken, j + 1)
                        wait(pe, k_heads_ready, j + 1)
                        wait(pe, shifted, j)
                        for half in range(2):
                            for b in range(PER_TILE):
                                last = nc.tensor.matmul(
                                    ps_s[b * SEQ:(b + 1) * SEQ, half * 512:(half + 1) * 512],
                                    q_t[:, u, b * SEQ:(b + 1) * SEQ],
                                    k_heads[:, u % 2, half * 8:(half + 1) * 8, b * SEQ:(b + 1) * SEQ],
                                    start=True, stop=True)
                        last.then_inc(scores_done, 1)
                    i, s = j - 5, (u - 5) % UNROLL
                    if on(i):
                        wait(pe, out_t_ready, i + 1)
                        wait(pe, y_taken, i)
                        nc.tensor.matmul(ps_y[:, 0:P], out_t[:, s % 2, :], wo, start=True, stop=True).then_inc(y_done, 1)
                    i, s = j - 3, (u - 3) % UNROLL
                    if on(i):
                        wait(pe, sums_taken, i + 1)
                        wait(pe, heads_ready, i)
                        wait(pe, in_t_taken, upto(j + 3))
                        for half in range(2):
                            last = nc.tensor.transpose(ps_in[:, (2 + half) * P:(3 + half) * P], sums_t[:, s % 2, half, :], t.ident[:, :])
                        last.then_inc(sums_back, 1)
                    i, s = j + 3, (u + 3) % UNROLL
                    if on(i):
                        wait(pe, norm_ready, i + 1)
                        wait(pe, in_t_taken, i)
                        wait(pe, heads_ready, j - 3)
                        for n in range(2):
                            last = nc.tensor.transpose(ps_in[:, n * P:(n + 1) * P], normed[:, s, n, :], t.ident[:, :])
                        last.then_inc(in_t_done, 1)
                    i, s = j - 4, u
                    if on(i):
                        wait(pe, heads_ready, i + 1)
                        wait(pe, out_t_ready, i)
                        wait(pe, sums_taken, upto(j - 2))
                        nc.tensor.transpose(ps_o[:, 2 * P:3 * P], heads_out[:, s % 2, :], t.ident[:, :]).then_inc(heads_t_done, 1)
                    i, s = j - 2, (u - 2) % UNROLL
                    if on(i):
                        wait(pe, prob_t_taken, i + 1)
                        wait(pe, sums_taken, i)
                        for b in range(PER_TILE):
                            for half in range(2):
                                for c in range(4):
                                    hp = 4 * half + c
                                    last = nc.tensor.matmul(
                                        ps_o[PAIR_COLS * c:PAIR_COLS * (c + 1), half * P + b * SEQ:half * P + (b + 1) * SEQ],
                                        t.v_by_pair[:, s, b * PAIRS + hp, :],
                                        prob_t[:, s % 2, hp, b * SEQ:(b + 1) * SEQ], start=True, stop=True)
                        last.then_inc(pv_done, 1)
                    i, s = j - 1, (u - 1) % UNROLL
                    if on(i):
                        wait(pe, exp_done, i + 1)
                        wait(pe, prob_t_taken, i)
                        for hp in range(PAIRS):
                            last = nc.tensor.transpose(ps_pt[:, hp * P:(hp + 1) * P],
                                                       prob[:, s % 2, hp * P:(hp + 1) * P], t.ident[:, :])
                        last.then_inc(prob_t_done, 1)
                    i, s = j + 2, (u + 2) % UNROLL
                    if on(i):
                        wait(pe, in_t_taken, i + 1)
                        wait(pe, qkv_taken, i)
                        nc.tensor.matmul(ps_qkv[:, P:2 * P], wk, turned[:, s % 2, 1, :], start=True, stop=True)
                        nc.tensor.matmul(ps_qkv[:, 0:P], wq, turned[:, s % 2, 0, :], start=True, stop=True)
                        for b in range(PER_TILE):
                            for h2 in range(2):
                                last = nc.tensor.matmul(
                                    ps_qkv[h2 * SEQ:(h2 + 1) * SEQ, 2 * P + b * SEQ:2 * P + (b + 1) * SEQ],
                                    turned[:, s % 2, 1, b * SEQ:(b + 1) * SEQ],
                                    wv[:, h2 * SEQ:(h2 + 1) * SEQ], start=True, stop=True)
                        last.then_inc(qkv_done, 1)
                    if isinstance(j, int) and j == T + 4:
                        wait(pe, shifted, T)
                        front_turn_in(nc, t, front, pe, 0, 0, ps_s[:, 0:CHUNK])

                steps.run(pe, step)

            @block.scalar
            def _(act):
                def step(j, u):
                    i, s = j + 3, (u + 3) % UNROLL
                    if on(i):
                        wait(act, in_t_done, i + 1)
                        wait(act, qkv_done, i - 1)
                        nc.scalar.activation(turned[:, s % 2, :, :], ps_in[:, 0:2 * P].rearrange("p (n d) -> p n d", n=2),
                                             ACT.Copy).then_inc(in_t_taken, 1)
                    i, s = j - 4, u
                    if on(i):
                        wait(act, heads_t_done, i + 1)
                        wait(act, pv_done, upto(j - 1))
                        wait(act, y_done, i - 1)
                        nc.scalar.activation(out_t[:, s % 2, :], ps_o[:, 2 * P:3 * P], ACT.Copy).then_inc(out_t_ready, 1)
                    i, s = j - 2, (u - 2) % UNROLL
                    if on(i):
                        wait(act, pv_done, i + 1)
                        wait(act, sums_back, i - 1)
                        nc.scalar.activation(sums_t[:, s % 2, :, :], ps_o[:, 0:2 * P].rearrange("p (n d) -> p n d", n=2),
                                             ACT.Copy).then_inc(sums_taken, 1)

                    i, s = j - 1, (u - 1) % UNROLL
                    if on(i):
                        wait(act, prob_t_done, i + 1)
                        wait(act, pv_done, i - 1)
                        nc.scalar.activation(prob_t[:, s % 2, :, :], ps_pt[:, :].rearrange("p (n d) -> p n d", n=PAIRS),
                                             ACT.Copy).then_inc(prob_t_taken, 1)
                    i, s = j + 2, (u + 2) % UNROLL
                    if on(i):
                        wait(act, qkv_done, i + 1)
                        wait(act, k_heads_ready, i - 3)
                        nc.scalar.activation(k_t[:, s, :], ps_qkv[:, P:2 * P], ACT.Identity,
                                             bias=t.qk_bias[:, layer, 1:2]).then_inc(k_taken, 1)
                        wait(act, scores_done, i - 3)
                        nc.scalar.activation(q_t[:, s, :], ps_qkv[:, 0:P], ACT.Identity,
                                             bias=t.qk_bias[:, layer, 0:1], scale=1.0)
                        wait(act, pv_done, i - 3)
                        for h2 in range(2):
                            rows = slice(h2 * SEQ, (h2 + 1) * SEQ)
                            last = nc.scalar.activation(
                                t.v_by_pair[rows, s, :, h2 * HEAD_DIM:(h2 + 1) * HEAD_DIM],
                                ps_qkv[rows, 2 * P:3 * P].rearrange("p (m d) -> p m d", d=HEAD_DIM), ACT.Copy)
                        last.then_inc(qkv_taken, 1)
                    i, s = j + 4, u
                    if on(i):
                        wait(act, offset_ready, i + 1)
                        wait(act, in_t_done, i - 3)
                        if gated:
                            wait(act, z_ready, i - 3)
                        src = (t.x[:, span(i, P)], t.ctx[:, span(i, P)])
                        for k in range(NORMS):
                            last = nc.scalar.activation(normed[:, s, k, :], src[k], ACT.Identity,
                                                        scale=rstd[:, s, k:k + 1], bias=offset[:, s, k:k + 1])
                        if not gated:
                            last = nc.scalar.activation(normed[:, s, 1, :], src[1], ACT.Copy)
                        last.then_inc(norm_ready, 1)
                    if on(j):
                        wait(act, shifted, j + 1)
                        nc.scalar.activation(prob[:, u % 2, :], prob[:, u % 2, :], ACT.Exp).then_inc(exp_done, 1)
                        if gated:
                            wait(act, z_ready, j + 1)
                            nc.scalar.activation(gate_exp[:, span(j, 1)], gate_in[:, u:u + 1], ACT.Exp, scale=-1.0,
                                                 bias=t.gate_nb[:, 0:1]).then_inc(gate_exp_ready, 1)
                    if gated and isinstance(j, int) and T + 4 <= j < T + 8:
                        n = j - T - 4
                        quarter = t.w_lo[:, :, :].rearrange("p g n -> p (g n)").bitcast(F32)[:, n * 11 * P:(n + 1) * 11 * P]
                        wait(act, lo_summed, n)
                        nc.scalar.activation(lo_abs[:, :], quarter, ACT.Abs, accum_out=t.lo_sum[:, n:n + 1]).then_inc(lo_summed, 1)
                    if isinstance(j, int) and j == T + 4:
                        front_take_in(nc, t, front, act, 0, 0, ps_s[:, 0:CHUNK])

                steps.run(act, step)

            @block.gpsimd
            def _(pool):
                def step(j, u):
                    i, s = j + 1, (u + 1) % UNROLL
                    if on(i):
                        wait(pool, k_taken, i + 1)
                        wait(pool, scores_done, i - 1)
                        nc.gpsimd.tensor_tensor(k_heads[:, s % 2, :, :],
                                                k_t[:, s, :].unsqueeze(1).to_broadcast([P, HEADS, P]),
                                                t.head_mask[:, :].unsqueeze(2).to_broadcast([P, HEADS, P]),
                                                ALU.mult).then_inc(k_heads_ready, 1)
                    i, s = j + 5, (u + 5) % UNROLL
                    first, last = NORMS, 0
                    if on(i):
                        wait(pool, spread_ready, i + 1)
                        wait(pool, norm_ready, i - 3)
                        first, last = 0, NORMS
                    if gated and on(j - 7):
                        wait(pool, y_spread_ready, j - 6)
                        wait(pool, x_done, j - 10)
                        last = 3
                    if last:
                        nc.gpsimd.tensor_tensor(rstd[:, s, first:last], spread[:, s, first:last], t.minus_half[:, first:last],
                                                ALU.pow).then_inc(rstd_ready, 1)
                    if on(j):
                        wait(pool, norm_ready, j + 1)
                        nc.gpsimd.tensor_tensor(t.x[:, span(j, P)], t.x[:, span(j, P)], closing_row, ALU.add).then_inc(biased, 1)
                    if isinstance(j, int) and j == T + 1:
                        front_power(nc, t, front, pool, 0, 0)

                steps.run(pool, step)

            @block.vector
            def _(dve):
                def step(j, u):
                    k, f = j, j + 5
                    b, slot_b = j - 6, (u - 6) % UNROLL
                    c, slot_c = j - 4, u
                    a, slot_a = j - 8, u
                    slot_f = (u + 5) % UNROLL
                    sums = ps_in[:, 2 * P:4 * P].rearrange("p (m r) -> p m r", r=PAIR_COLS)
                    if gated and on(b):
                        wait(dve, y_done, b + 1)
                        wait(dve, x_done, b - 3)
                        nc.vector.tensor_tensor(y[:, slot_b, :], ps_y[:, 0:P], t.bias_row[:, 0, :], ALU.add).then_inc(y_taken, 1)
                    if not gated and on(b):
                        wait(dve, y_done, b + 1)
                        wait(dve, biased, b + 1)
                        nc.vector.tensor_tensor(t.x[:, span(b, P)], ps_y[:, 0:P], t.x[:, span(b, P)], ALU.add).then_inc(y_taken, 1)
                    if on(c):
                        wait(dve, sums_back, c + 1)
                        wait(dve, in_t_taken, upto(j + 3))
                        nc.vector.reciprocal(rden[:, slot_c % 2, :, :], sums[:, :, 2 * HEAD_DIM:2 * HEAD_DIM + 2]).then_inc(rden_ready, 1)
                    if gated and on(b):
                        wait(dve, gate_exp_ready, b + 1)
                        nc.vector.tensor_scalar(gate[:, slot_b:slot_b + 1], gate_exp[:, span(b, 1)], 1.0, None, ALU.add).then_inc(y_chain, 1)
                        wait(dve, y_taken, b + 1)
                        nc.vector.bn_stats(y_stats[:, :], y[:, slot_b, :]).then_inc(y_chain, 1)
                    if on(c):
                        wait(dve, rden_ready, c + 1)
                        wait(dve, heads_t_done, c - 1)
                        nc.vector.tensor_tensor(heads_out[:, slot_c % 2, :].rearrange("p (m h d) -> p m h d", h=2, d=HEAD_DIM),
                                                sums[:, :, 0:2 * HEAD_DIM].rearrange("p m (h d) -> p m h d", d=HEAD_DIM),
                                                rden[:, slot_c % 2, :, :].unsqueeze(3).to_broadcast([P, PAIRS, 2, HEAD_DIM]),
                                                ALU.mult).then_inc(heads_ready, 1)
                    if gated and on(b):
                        wait(dve, y_chain, 5 * b + 2)
                        nc.vector.reciprocal(gate[:, slot_b:slot_b + 1], gate[:, slot_b:slot_b + 1]).then_inc(y_chain, 1)
                        nc.vector.bn_aggr(y_moments[:, slot_b, :], y_stats[:, :]).then_inc(y_chain, 1)
                    if gated and on(a):
                        wait(dve, rstd_ready, rstd_step(j - 1))
                        wait(dve, x_done, a)
                        nc.vector.tensor_tensor(y_scale[:, 0:1], rstd[:, slot_a, 2:3], gate[:, slot_a:slot_a + 1], ALU.mult)
                        nc.vector.scalar_tensor_tensor(out=y_gain[:, :], in0=y[:, slot_a, :], scalar=y_moments[:, slot_a, 0:1],
                                                       in1=t.ln_o_g[:, :], op0=ALU.subtract, op1=ALU.mult).then_inc(y2_chain, 1)
                    if gated and on(b):
                        wait(dve, y_chain, 5 * b + 4)
                        nc.vector.scalar_tensor_tensor(out=y_tmp[:, slot_b:slot_b + 1], in0=y_moments[:, slot_b, 1:2], scalar=gate[:, slot_b:slot_b + 1],
                                                       in1=gate[:, slot_b:slot_b + 1], op0=ALU.mult, op1=ALU.mult).then_inc(y_chain, 1)
                    if gated and on(j + 1):
                        wait(dve, norm_ready, j + 2)
                        wait(dve, z_ready, j + 1)
                        wait(dve, gate_exp_ready, j - 2)
                        nc.vector.tensor_tensor_reduce(out=gate_prod[:, :], in0=normed[:, (u + 1) % UNROLL, 0, :], in1=t.gate_w[:, :],
                                                       scale=1.0, scalar=0.0, op0=ALU.mult, op1=ALU.add,
                                                       accum_out=gate_in[:, (u + 1) % UNROLL:(u + 1) % UNROLL + 1]).then_inc(z_ready, 1)
                    if gated and isinstance(f, int) and f in t.load_steps:
                        wait(dve, t.tiles_loaded[t.load_steps.index(f)], 32)
                    if on(f):
                        src = (t.x[:, span(f, P)], t.ctx[:, span(f, P)])
                        for n in range(NORMS):
                            last = nc.vector.bn_stats(stats[:, slot_f, n, :], src[n])
                        last.then_inc(ln_chain, 1)
                    if gated and on(a):
                        wait(dve, y2_chain, a + 1)
                        wait(dve, biased, a + 1)
                        nc.vector.scalar_tensor_tensor(out=t.x[:, span(a, P)], in0=y_gain[:, :], scalar=y_scale[:, 0:1],
                                                       in1=t.x[:, span(a, P)], op0=ALU.mult, op1=ALU.add).then_inc(x_done, 1)
                    if gated and on(b):
                        wait(dve, y_chain, 5 * b + 5)
                        wait(dve, rstd_ready, rstd_step(j - 3))
                        nc.vector.tensor_scalar(spread[:, slot_b, 2:3], y_tmp[:, slot_b:slot_b + 1], EPS, None,
                                                ALU.add).then_inc(y_spread_ready, 1)
                    if on(k):
                        if on(f):
                            wait(dve, ln_chain, 2 * f + 1)
                            wait(dve, offset_ready, f - 3)
                        wait(dve, scores_done, k + 1)
                        nc.vector.tensor_reduce(out=top[:, u % 2, :], in_=ps_s[:, :].rearrange("p (h k) -> p h k", h=HEADS),
                                                op=ALU.max, axis=AX.X).then_inc(top_ready, 1)
                    if on(f):
                        if not on(k):
                            wait(dve, ln_chain, 2 * f + 1)
                            wait(dve, offset_ready, f - 3)
                        for n in range(NORMS):
                            last = nc.vector.bn_aggr(moments[:, slot_f, n, :], stats[:, slot_f, n, :])
                        last.then_inc(ln_chain, 1)
                    if on(j + 4):
                        wait(dve, rstd_ready, rstd_step(j - 1))
                        wait(dve, norm_ready, j + 1)
                        nc.vector.scalar_tensor_tensor(out=offset[:, u, 0:NORMS], in0=moments[:, u, 0:NORMS, 0], scalar=-1.0,
                                                       in1=rstd[:, u, 0:NORMS], op0=ALU.mult, op1=ALU.mult).then_inc(offset_ready, 1)
                    if on(f):
                        wait(dve, ln_chain, 2 * f + 2)
                        wait(dve, rstd_ready, rstd_step(j - 4))
                        if gated:
                            nc.vector.tensor_scalar(spread[:, slot_f, 0:1], moments[:, slot_f, 0, 1:2], 1.0 + EPS, EPS * EPS, ALU.mult, ALU.add)
                            nc.vector.tensor_scalar(spread[:, slot_f, 1:2], moments[:, slot_f, 1, 1:2], EPS, None, ALU.add).then_inc(spread_ready, 1)
                        else:
                            nc.vector.tensor_scalar(spread[:, slot_f, 0:1], moments[:, slot_f, 0, 1:2], EPS, None, ALU.add).then_inc(spread_ready, 1)
                    if on(k):
                        wait(dve, top_ready, k + 1)
                        wait(dve, prob_t_done, k - 1)
                        nc.vector.tensor_tensor(prob[:, u % 2, :].rearrange("p (h k) -> p h k", h=HEADS),
                                                ps_s[:, :].rearrange("p (h k) -> p h k", h=HEADS),
                                                top[:, u % 2, :].unsqueeze(2).to_broadcast([P, HEADS, SEQ]),
                                                ALU.subtract).then_inc(shifted, 1)
                    if isinstance(j, int) and j == T:
                        wait(dve, x_done if gated else y_taken, CHUNK_TILES)
                        front_measure(nc, t, front, dve, 0, 0)
                    if isinstance(j, int) and j == T + 1:
                        front_moments(nc, t, front, dve, 0, 0)
                        front_spread(nc, t, front, dve, 0, 0)
                    if isinstance(j, int) and j == T + 3:
                        front_normalise(nc, t, front, dve, 0, 0)
                    if isinstance(j, int) and j == T + 7:
                        front_split_in(nc, t, front, dve, 0, 0, ps_s[:, 0:CHUNK])

                steps.run(dve, step)


def split_products(nc, out, w_hi, w_lo, x_hi, x_lo, first, last):
    if w_lo is not None:
        nc.tensor.matmul(out, w_lo, x_hi, start=first, stop=False)
    nc.tensor.matmul(out, w_hi, x_lo, start=first and w_lo is None, stop=False)
    return nc.tensor.matmul(out, w_hi, x_hi, start=False, stop=last)


def gated_feed_forward(nc, t, front):
    N = t.tiles // CHUNK_TILES
    steps = Steps(N, lead=2, lag=2, unroll=1)
    on = steps.on

    def ahead(i):
        return on(i) and not (isinstance(i, int) and i == 0)
    LEVELS = 3

    with ExitStack() as ctx:
        def sb(name, shape, dt=F32):
            return ctx.enter_context(nc.sbuf_tensor(f"g_{name}", shape, dt))

        def psum(name, n=1):
            return ctx.enter_context(nc.psum_tensor(f"g_{name}", [P, 512 * n], F32))

        def sem(name):
            return ctx.enter_context(nc.semaphore(f"g_{name}"))

        h = sb("h", [P, 2, CHUNK])
        silu = sb("silu", [P, 2, CHUNK])
        h_hi = [sb(f"h_hi{n}", [P, 4, CHUNK], F32R) for n in range(LEVELS)]
        h_lo = [sb(f"h_lo{n}", [P, 4, CHUNK], F32R) for n in range(LEVELS)]
        out_t = sb("out_t", [P, CHUNK])
        lo_max = sb("lo_max", [P, 1])
        lo_bits_row = sb("lo_bits", [1, 1])

        ps = psum("ps", 6)
        ps_in = psum("ps_in")
        ps_out = psum("ps_out")

        lo_sum_ready = sem("lo_sum_ready")
        lo_row_ready = sem("lo_row_ready")
        lo_bits_ready = sem("lo_bits_ready")
        done = [front.up_done, sem("done1"), sem("done2")]
        silu_ready = sem("silu_ready")
        act_ready = [sem(f"act_ready{n}") for n in range(LEVELS)]
        hi_ready = [sem(f"hi_ready{n}") for n in range(LEVELS)]
        lo_ready = [sem(f"lo_ready{n}") for n in range(LEVELS)]
        out_done = sem("out_done")
        out_taken = sem("out_taken")
        back_done = sem("back_done")
        x_done = sem("x_done")

        def bank(n):
            return ps[:, n * 512:(n + 1) * 512]

        def pair(o):
            return (4, 0, 2, 4)[o]

        with nc.Block() as block:
            @block.tensor
            def _(pe):
                def program(with_lo):
                    def w(g, cols):
                        return t.w_hi[:, g, cols], t.w_lo[:, g, cols] if with_lo else None

                    def up(i, outputs):
                        if not on(i):
                            return
                        wait(pe, front.x_lo_ready, i + 1)
                        for o in outputs:
                            wait(pe, *((act_ready[0], 4 * i), (act_ready[1], 4 * i - 2),
                                       (act_ready[1], 4 * i), (act_ready[0], 4 * i + 1))[o])
                            for g in range(2):
                                last = split_products(nc, bank(pair(o) + g), *w(g, slice(o * P, (o + 1) * P)),
                                                      front.x_hi[:, 0, :], front.x_lo[:, 0, :], True, True)
                            last.then_inc(done[0], 1)

                    def middle(i, level):
                        if not on(i):
                            return
                        wait(pe, lo_ready[level - 1], 4 * i + 4)
                        for o in range(4):
                            if level == 1:
                                wait(pe, act_ready[2], 4 * (i - 1) + o + 1)
                            elif isinstance(i, int) and i + 1 >= N:
                                wait(pe, act_ready[1], 4 * i + o + 1)
                            else:
                                wait(pe, act_ready[0], 4 * (i + 1) + (2 if o < 2 else 3))
                            for c in range(4):
                                last = split_products(nc, bank(o), *w(2 + 4 * (level - 1) + c, slice(o * P, (o + 1) * P)),
                                                      h_hi[level - 1][:, c, :], h_lo[level - 1][:, c, :], c == 0, c == 3)
                            last.then_inc(done[level], 1)

                    def down(i):
                        if not on(i):
                            return
                        wait(pe, lo_ready[LEVELS - 1], 4 * i + 4)
                        wait(pe, x_done, i)
                        for c in range(4):
                            last = split_products(nc, ps_out[:, :], *w(10, slice(c * P, (c + 1) * P)),
                                                  h_hi[LEVELS - 1][:, c, :], h_lo[LEVELS - 1][:, c, :], c == 0, c == 3)
                        last.then_inc(out_done, 1)

                    def turn_back(i):
                        if on(i):
                            wait(pe, out_taken, i + 1)
                            for k in range(CHUNK_TILES):
                                last = nc.tensor.transpose(ps_out[:, k * P:(k + 1) * P], out_t[:, k * P:(k + 1) * P], t.ident[:, :])
                            last.then_inc(back_done, 1)

                    def step(j, u):
                        if ahead(j + 1):
                            front_turn_in(nc, t, front, pe, j + 1, 0, ps_in)
                        middle(j, 1)
                        up(j + 1, (0, 1))
                        down(j - 1)
                        up(j + 1, (2, 3))
                        turn_back(j - 1)
                        middle(j, 2)

                    steps.run(pe, step)

                pe.wait_ge(lo_sum_ready, 1)
                nc.tensor.transpose(ps_in[0:1, 0:P], lo_max[:, :], t.ident[:, :]).then_inc(lo_row_ready, 1)
                pe.wait_ge(lo_bits_ready, 1)
                lo_bits = pe.value_load(lo_bits_row[0:1, 0:1].bitcast(I32))
                with pe.If(lo_bits):
                    program(with_lo=True)
                with pe.Else():
                    program(with_lo=False)

            @block.scalar
            def _(act):
                def hidden(i, level):
                    if not on(i):
                        return
                    for o in range(4):
                        wait(act, done[level], 4 * i + o + 1)
                        wait(act, lo_ready[level], 4 * i + o - 1)
                        if o < 2:
                            if level == 1:
                                wait(act, lo_ready[2], 4 * i)
                            elif isinstance(i, int) and i + 1 >= N:
                                wait(act, lo_ready[1], 4 * i + 4)
                            else:
                                wait(act, lo_ready[0], 4 * i + 8)
                        nc.scalar.activation(h[:, o % 2, :], bank(o), ACT.Gelu,
                                             scale=t.s[:, 1 + level, o:o + 1]).then_inc(act_ready[level], 1)
                        split_hi(i, level, o)

                def split_hi(i, level, o):
                    wait(act, act_ready[level], 4 * i + o + 1)
                    wait(act, *readers(i, level))
                    nc.scalar.activation(h_hi[level][:, o, :], h[:, o % 2, :], ACT.Copy).then_inc(hi_ready[level], 1)

                def readers(i, level):
                    if level == LEVELS - 1:
                        return out_done, i
                    return done[level + 1], 4 * i

                def take_out(i):
                    if on(i):
                        wait(act, out_done, i + 1)
                        wait(act, back_done, i)
                        nc.scalar.activation(out_t[:, :], ps_out[:, :], ACT.Copy, scale=t.s3[:, 0:1]).then_inc(out_taken, 1)

                def silu_stage(i, after):
                    if not on(i):
                        take_out(after)
                        return
                    for o in range(4):
                        wait(act, done[0], 4 * i + o + 1)
                        wait(act, act_ready[0], 4 * i + o - 1)
                        nc.scalar.activation(silu[:, o % 2, :], bank(pair(o)), ACT.Silu,
                                             scale=t.s[:, 0, o:o + 1]).then_inc(silu_ready, 1)
                        if o > 0:
                            split_hi(i, 0, o - 1)
                        if o == 1:
                            take_out(after)
                    split_hi(i, 0, 3)

                def step(j, u):
                    if ahead(j + 1):
                        front_take_in(nc, t, front, act, j + 1, 0, ps_in[:, :])
                    hidden(j, 1)
                    silu_stage(j + 1, after=j - 1)
                    hidden(j, 2)

                wait(act, t.scales_loaded, 16 * 7)
                steps.run(act, step)

            @block.gpsimd
            def _(pool):
                def step(j, u):
                    if ahead(j + 2):
                        front_power(nc, t, front, pool, j + 2, 0)

                steps.run(pool, step)

            @block.vector
            def _(dve):
                def split_lo(i, level, o):
                    wait(dve, hi_ready[level], 4 * i + o + 1)
                    nc.vector.tensor_tensor(h_lo[level][:, o, :], h[:, o % 2, :], h_hi[level][:, o, :].bitcast(F32),
                                            ALU.subtract).then_inc(lo_ready[level], 1)

                def product_stage(i):
                    if not on(i):
                        return
                    for o in range(4):
                        wait(dve, silu_ready, 4 * i + o + 1)
                        wait(dve, *((lo_ready[0], 4 * i + o - 1) if o > 1 else (lo_ready[1], 4 * i)))
                        nc.vector.scalar_tensor_tensor(out=h[:, o % 2, :], in0=bank(pair(o) + 1), scalar=t.s[:, 1, o:o + 1],
                                                       in1=silu[:, o % 2, :], op0=ALU.mult, op1=ALU.mult).then_inc(act_ready[0], 1)
                        if o > 0:
                            split_lo(i, 0, o - 1)
                    split_lo(i, 0, 3)

                def residual(i):
                    if on(i):
                        wait(dve, back_done, i + 1)
                        nc.vector.tensor_tensor(t.x[:, span(i, CHUNK)], ps_out[:, :], t.x[:, span(i, CHUNK)], ALU.add).then_inc(x_done, 1)

                def step(j, u):
                    if ahead(j + 1):
                        front_split_in(nc, t, front, dve, j + 1, 0, ps_in[:, :])
                    if ahead(j + 2):
                        front_measure(nc, t, front, dve, j + 2, 0)
                    if on(j):
                        split_lo(j, 1, 0)
                    if ahead(j + 2):
                        front_moments(nc, t, front, dve, j + 2, 0)
                        front_spread(nc, t, front, dve, j + 2, 0)
                    if on(j):
                        for o in range(1, 4):
                            split_lo(j, 1, o)
                    product_stage(j + 1)
                    residual(j - 1)
                    if ahead(j + 2):
                        front_normalise(nc, t, front, dve, j + 2, 0)
                    if on(j):
                        for o in range(4):
                            split_lo(j, 2, o)

                wait(dve, t.scales_loaded, 16 * 7)
                nc.vector.tensor_reduce(out=lo_max[:, :], in_=t.lo_sum[:, :], op=ALU.max, axis=AX.X).then_inc(lo_sum_ready, 1)
                dve.wait_ge(lo_row_ready, 1)
                nc.vector.tensor_reduce(out=lo_bits_row[:, :], in_=ps_in[0:1, 0:P], op=ALU.max, axis=AX.X).then_inc(lo_bits_ready, 1)
                steps.run(dve, step)


def plain_feed_forward(nc, t, front):
    N = t.tiles // CHUNK_TILES
    steps = Steps(N, lead=3, lag=3, unroll=2)
    on = steps.on

    def ahead(i):
        return on(i) and not (isinstance(i, int) and i == 0)

    with ExitStack() as ctx:
        def sb(name, shape, dt=F32):
            return ctx.enter_context(nc.sbuf_tensor(f"p_{name}", shape, dt))

        def psum(name, n=1):
            return ctx.enter_context(nc.psum_tensor(f"p_{name}", [P, 512 * n], F32))

        def sem(name):
            return ctx.enter_context(nc.semaphore(f"p_{name}"))

        h = sb("h", [P, 4, CHUNK])
        h_hi, h_lo = sb("h_hi", [P, 2, 4, CHUNK], F32R), sb("h_lo", [P, 2, 4, CHUNK], F32R)
        out_t = sb("out_t", [P, 2, CHUNK])

        ps = psum("ps", 4)
        ps_in = psum("ps_in")
        ps_out = psum("ps_out", 2)
        ps_back = psum("ps_back")

        up_done = front.up_done
        h_ready = sem("h_ready")
        hi_ready = sem("hi_ready")
        lo_ready = sem("lo_ready")
        out_done = sem("out_done")
        out_taken = sem("out_taken")
        back_done = sem("back_done")
        x_done = sem("x_done")
        stored = sem("stored")

        def bank(of, n):
            return of[:, n * 512:(n + 1) * 512]

        with nc.Block() as block:
            @block.tensor
            def _(pe):
                def step(j, u):
                    if on(j):
                        wait(pe, front.x_lo_ready, j + 1)
                        for o in range(4):
                            cols = slice(o * P, (o + 1) * P)
                            wait(pe, h_ready, 4 * (j - 1) + o + 1)
                            last = split_products(nc, bank(ps, o), t.f1_hi[:, 0, cols], t.f1_lo[:, 0, cols],
                                                  front.x_hi[:, u, :], front.x_lo[:, u, :], True, True)
                            last.then_inc(up_done, 1)
                    if ahead(j + 1):
                        front_turn_in(nc, t, front, pe, j + 1, 1 - u, ps_in)
                    i, s = j - 1, 1 - u
                    if on(i):
                        wait(pe, lo_ready, 4 * i + 4)
                        wait(pe, out_taken, i - 1)
                        for c in range(4):
                            cols = slice(c * P, (c + 1) * P)
                            last = split_products(nc, bank(ps_out, s), t.f1_hi[:, 1, cols], t.f1_lo[:, 1, cols],
                                                  h_hi[:, s, c, :], h_lo[:, s, c, :], c == 0, c == 3)
                        last.then_inc(out_done, 1)
                    i, s = j - 2, u
                    if on(i):
                        wait(pe, out_taken, i + 1)
                        wait(pe, x_done, i)
                        for k in range(CHUNK_TILES):
                            last = nc.tensor.transpose(ps_back[:, k * P:(k + 1) * P], out_t[:, s, k * P:(k + 1) * P], t.ident[:, :])
                        last.then_inc(back_done, 1)

                steps.run(pe, step)

            @block.scalar
            def _(act):
                def step(j, u):
                    i, s = j - 2, u
                    if on(i):
                        wait(act, out_done, i + 1)
                        wait(act, back_done, i - 1)
                        nc.scalar.activation(out_t[:, s, :], bank(ps_out, s), ACT.Identity, bias=t.b2[:, 0:1]).then_inc(out_taken, 1)
                    if on(j):
                        wait(act, out_done, j - 1)
                    for o in range(5):
                        if on(j) and o < 4:
                            wait(act, up_done, 4 * j + o + 1)
                            wait(act, lo_ready, 4 * j + o - 3)
                            nc.scalar.activation(h[:, o, :], bank(ps, o), ACT.Relu, bias=t.b1[:, o:o + 1]).then_inc(h_ready, 1)
                        if on(j) and o > 0:
                            wait(act, h_ready, 4 * j + o)
                            nc.scalar.activation(h_hi[:, u, o - 1, :], h[:, o - 1, :], ACT.Copy).then_inc(hi_ready, 1)
                        if ahead(j + 1) and o == 2:
                            front_take_in(nc, t, front, act, j + 1, 1 - u, ps_in[:, :])

                steps.run(act, step)

            @block.gpsimd
            def _(pool):
                def step(j, u):
                    if ahead(j + 3):
                        front_power(nc, t, front, pool, j + 3, 1 - u)

                steps.run(pool, step)

            @block.vector
            def _(dve):
                def split_lo(i, s, o):
                    wait(dve, hi_ready, 4 * i + o + 1)
                    nc.vector.tensor_tensor(h_lo[:, s, o, :], h[:, o, :], h_hi[:, s, o, :].bitcast(F32),
                                            ALU.subtract).then_inc(lo_ready, 1)

                def step(j, u):
                    i, s = j - 3, 1 - u
                    if on(i):
                        wait(dve, back_done, i + 1)
                        nc.vector.tensor_tensor(t.x[:, span(i, CHUNK)], ps_back[:, :], t.x[:, span(i, CHUNK)], ALU.add).then_inc(x_done, 1)
                    f, s = j + 3, 1 - u
                    if ahead(f):
                        front_measure(nc, t, front, dve, f, s)
                    if on(j):
                        wait(dve, out_done, j - 1)
                        split_lo(j, u, 0)
                    if ahead(f):
                        front_moments(nc, t, front, dve, f, s)
                    if on(j):
                        split_lo(j, u, 1)
                    if ahead(f):
                        front_spread(nc, t, front, dve, f, s)
                    if ahead(j + 1):
                        front_split_in(nc, t, front, dve, j + 1, 1 - u, ps_in[:, :])
                    if ahead(j + 2):
                        front_normalise(nc, t, front, dve, j + 2, u)
                    if on(j):
                        split_lo(j, u, 2)
                        split_lo(j, u, 3)

                steps.run(dve, step)

            @block.sync
            def _(sp):
                xs = t.x[:, :].rearrange("p (t d) -> p t d", d=P)
                with sp.Fori(0, N) as i:
                    wait(sp, x_done, i + 1)
                    sp.dma_start(t.out.rearrange("(t b) s d -> (b s) t d", b=PER_TILE)[:, bass.ds(i * CHUNK_TILES, CHUNK_TILES), :],
                                 xs[:, bass.ds(i * CHUNK_TILES, CHUNK_TILES), :]).then_inc(stored, 16)
                sp.wait_ge(stored, 16 * N)


class Tensors:
    pass


def two_layer_xattn_ffn(nc, a, out):
    with ExitStack() as ctx:
        def sb(name, shape, dt=F32):
            return ctx.enter_context(nc.sbuf_tensor(name, shape, dt))

        t = Tensors()
        t.out = out
        t.tiles = a["x"].shape[0] // PER_TILE
        t.x = sb("x_res", [P, t.tiles * P])
        t.ctx = sb("ctx_res", [P, t.tiles * P])
        t.ident = sb("ident", [P, P])
        t.head_mask = sb("head_mask", [P, HEADS])
        t.minus_half = sb("minus_half", [P, 4])
        t.v_by_pair = sb("v_by_pair", [P, UNROLL, PER_TILE * PAIRS, PAIR_COLS])
        t.wa = sb("wa", [P, 2, 4, P])
        t.qk_bias = sb("qk_bias", [P, 2, 2])
        t.bias_row = sb("bias_row", [P, 2, P])
        t.ln_o_g = sb("ln_o_g", [P, P])
        t.ln_o_b = sb("ln_o_b", [P, P])
        t.gate_w = sb("gate_w", [P, P])
        t.gate_nb = sb("gate_nb", [P, 1])
        t.w_hi = sb("w_hi", [P, 11, 512], F32R)
        t.w_lo = sb("w_lo", [P, 11, 512], F32R)
        t.lo_sum = sb("lo_sum", [P, 4])
        t.f1_hi = sb("f1_hi", [P, 2, 512], F32R)
        t.f1_lo = sb("f1_lo", [P, 2, 512], F32R)
        t.scales_loaded = ctx.enter_context(nc.semaphore("scales_loaded"))
        t.load_steps = [0, 8, 16]
        t.tiles_loaded = [ctx.enter_context(nc.semaphore(f"tiles_loaded{n}")) for n in range(len(t.load_steps))]
        t.s = sb("s", [P, 4, 4])
        t.s3 = sb("s3", [P, 1])
        t.b1 = sb("b1", [P, 4])
        t.b2 = sb("b2", [P, 1])

        prepare(nc, t, a)
        with ExitStack() as layer:
            front = Front(nc, layer, "front0", slots=1)
            attention(nc, t, 0, front)
            gated_feed_forward(nc, t, front)
        with ExitStack() as layer:
            front = Front(nc, layer, "front1", slots=2)
            attention(nc, t, 1, front)
            plain_feed_forward(nc, t, front)


def kernel(**inputs):
    import numpy as np
    import concourse.bacc as bacc
    from concourse.bass_utils import run_bass_kernel_spmd

    nc = bacc.Bacc("TRN2", target_bir_lowering=False, num_devices=1)
    arrays, args = {}, {}
    for name, value in inputs.items():
        array = np.ascontiguousarray(value)
        arrays[f"in_{name}"] = array
        args[name] = nc.dram_tensor(f"in_{name}", array.shape, mybir.dt.from_np(array.dtype), kind="ExternalInput").ap()
    x = inputs["x"]
    out = nc.dram_tensor("out_x", x.shape, F32, kind="ExternalOutput").ap()
    two_layer_xattn_ffn(nc, args, out)
    r = run_bass_kernel_spmd(nc, [arrays], core_ids=[0])
    return r.results[0]["out_x"]
```
